# Optimizing a Trainium2 kernel written in Bass

```python
import numpy as np
import jax
import jax.numpy as jnp

def _softmax(x, axis=-1):
    return jax.nn.softmax(x, axis=axis)

def _gelu(x):
    return jax.nn.gelu(x, approximate=True)

def _silu(x):
    return jax.nn.silu(x)

def _sigmoid(x):
    return jax.nn.sigmoid(x)

def _layernorm(x, axis=-1, eps=1e-05):
    m = jnp.mean(x, axis=axis, keepdims=True)
    v = jnp.var(x, axis=axis, keepdims=True)
    return (x - m) / jnp.sqrt(v + eps)

def _scatter_add(tgt, idx, src, axis=0):
    return tgt.at[idx].add(src)

def _segment_sum(src, seg, n):
    return jax.ops.segment_sum(src, seg, n)
kernel_name = 'mk_adj_seq_d1_adj_r2_39fcec'

def setup_inputs(seed: int=0):
    np.random.seed(seed)
    _w = jnp.asarray

    def _rec_inputs():
        import jax
        import jax.numpy as jnp
        _gk = jax.random.key(seed)
        x = 0.0003765 + 1 * jax.random.normal(jax.random.fold_in(_gk, 1), (64, 128, 256), jnp.float32)
        _w = (1.0 + jnp.arange(128, dtype=jnp.float32)) ** (-0.5)
        _w = _w / _w.mean()
        _pij = jnp.clip(0.0625 * _w[:, None] * _w[None, :], 0.0, 1.0)
        _a = jax.random.uniform(jax.random.fold_in(_gk, 2), (64, 128, 128)) < _pij
        adj = _a.astype(jnp.int32)
        return (x, adj)
    x, adj = _rec_inputs()

    def _L0_gnn_setup():
        import jax, jax.numpy as jnp
        import numpy as np
        B, N, H, D = (8, 512, 256, 4)
        EPS = 1e-08
        LN_EPS = 1e-05

        def _linear(x, W, b):
            return x @ W.T + b
        key = jax.random.key(seed)
        ks = jax.random.split(key, 20)
        inp = {'adj': jax.random.randint(ks[0], (B, N, N), 0, D + 1, dtype=jnp.int32), 'relative_pos': jax.random.randint(ks[1], (B, N, N), 0, 16, dtype=jnp.int32), 'hid': jax.random.normal(ks[2], (B, N, H), dtype=jnp.float32), 'Wd': jax.random.normal(ks[3], (H, D * H), dtype=jnp.float32) * (1.0 / np.sqrt(D * H)), 'bd': jnp.zeros((H,), jnp.float32)}
        s = 1.0 / np.sqrt(H)
        for i, nm in enumerate(['ri', 'rh', 'zi', 'zh', 'ni', 'nh']):
            inp['W' + nm] = jax.random.normal(ks[4 + i], (H, H), dtype=jnp.float32) * s
            inp['b' + nm] = jnp.zeros((H,), jnp.float32)
        inp['gamma'] = jnp.ones((H,), jnp.float32)
        inp['beta'] = jnp.zeros((H,), jnp.float32)
        return inp
    _L0_gnn_all = _L0_gnn_setup()
    _L0_gnn_in = {k: v for k, v in _L0_gnn_all.items() if k in ('Wd', 'bd', 'Wri', 'bri', 'Wrh', 'brh', 'Wzi', 'bzi', 'Wzh', 'bzh', 'Wni', 'bni', 'Wnh', 'bnh', 'gamma', 'beta')}
    del _L0_gnn_all
    return {'x': x, 'adj': adj, 'L0_gnn_Wd': _L0_gnn_in['Wd'], 'L0_gnn_bd': _L0_gnn_in['bd'], 'L0_gnn_Wri': _L0_gnn_in['Wri'], 'L0_gnn_bri': _L0_gnn_in['bri'], 'L0_gnn_Wrh': _L0_gnn_in['Wrh'], 'L0_gnn_brh': _L0_gnn_in['brh'], 'L0_gnn_Wzi': _L0_gnn_in['Wzi'], 'L0_gnn_bzi': _L0_gnn_in['bzi'], 'L0_gnn_Wzh': _L0_gnn_in['Wzh'], 'L0_gnn_bzh': _L0_gnn_in['bzh'], 'L0_gnn_Wni': _L0_gnn_in['Wni'], 'L0_gnn_bni': _L0_gnn_in['bni'], 'L0_gnn_Wnh': _L0_gnn_in['Wnh'], 'L0_gnn_bnh': _L0_gnn_in['bnh'], 'L0_gnn_gamma': _L0_gnn_in['gamma'], 'L0_gnn_beta': _L0_gnn_in['beta']}

def reference(x, adj, L0_gnn_Wd, L0_gnn_bd, L0_gnn_Wri, L0_gnn_bri, L0_gnn_Wrh, L0_gnn_brh, L0_gnn_Wzi, L0_gnn_bzi, L0_gnn_Wzh, L0_gnn_bzh, L0_gnn_Wni, L0_gnn_bni, L0_gnn_Wnh, L0_gnn_bnh, L0_gnn_gamma, L0_gnn_beta):
    import jax
    import jax.numpy as jnp

    def _L0_gnn_ref(adj, relative_pos, hid, Wd, bd, Wri, bri, Wrh, brh, Wzi, bzi, Wzh, bzh, Wni, bni, Wnh, bnh, gamma, beta):
        import jax, jax.numpy as jnp
        import numpy as np
        B, N, H, D = (8, 512, 256, 4)
        EPS = 1e-08
        LN_EPS = 1e-05

        def _linear(x, W, b):
            return x @ W.T + b
        dt = hid.dtype
        labels = jnp.arange(1, D + 1, dtype=adj.dtype)
        mask = (adj[None] == labels[:, None, None, None]).astype(dt)
        weight = mask / (jnp.sum(mask, axis=-1, keepdims=True) + EPS)
        agg = jnp.einsum('dbmn,bnh->bmdh', weight, hid).reshape(hid.shape[0], hid.shape[1], D * H)
        out = jax.nn.relu(_linear(agg, Wd, bd))
        r = jax.nn.sigmoid(_linear(out, Wri, bri) + _linear(hid, Wrh, brh))
        z = jax.nn.sigmoid(_linear(out, Wzi, bzi) + _linear(hid, Wzh, bzh))
        n = jnp.tanh(_linear(out, Wni, bni) + r * _linear(hid, Wnh, bnh))
        out = (1.0 - z) * n + z * hid
        mu = jnp.mean(out, axis=-1, keepdims=True)
        var = jnp.var(out, axis=-1, keepdims=True)
        return (out - mu) / jnp.sqrt(var + LN_EPS) * gamma + beta
    x = _L0_gnn_ref(adj, adj, x, L0_gnn_Wd, L0_gnn_bd, L0_gnn_Wri, L0_gnn_bri, L0_gnn_Wrh, L0_gnn_brh, L0_gnn_Wzi, L0_gnn_bzi, L0_gnn_Wzh, L0_gnn_bzh, L0_gnn_Wni, L0_gnn_bni, L0_gnn_Wnh, L0_gnn_bnh, L0_gnn_gamma, L0_gnn_beta)
    return x

_drawn_inputs = setup_inputs


def setup_inputs(seed=0):
    import zlib

    import numpy as np

    out = dict(_drawn_inputs(seed))
    spreads = {'L0_gnn_bd': (0.0, 0.1),
     'L0_gnn_bri': (0.0, 0.66),
     'L0_gnn_brh': (0.0, 0.615),
     'L0_gnn_bzi': (0.0, 0.1),
     'L0_gnn_bzh': (0.0, 0.1),
     'L0_gnn_bni': (0.0, 0.1),
     'L0_gnn_bnh': (0.0, 0.1),
     'L0_gnn_gamma': (1.0, 0.2),
     'L0_gnn_beta': (0.0, 0.1)}
    factors = {'L0_gnn_Wri': 2.797}
    for name, (base, spread) in spreads.items():
        noise = np.random.default_rng([zlib.crc32(name.encode()), seed]).standard_normal(out[name].shape)
        drawn = base * np.exp(spread * noise) if base else spread * noise
        out[name] = jnp.asarray(drawn.astype(out[name].dtype))
    for name, factor in factors.items():
        out[name] = (out[name] * factor).astype(out[name].dtype)
    return out
```

```python
import concourse.bass as bass
from concourse import mybir
from contextlib import ExitStack

GRAPHS, N, H, D = 64, 128, 256, 4
EPS, LN_EPS = 1e-8, 1e-5
GROUP = 4
HC = H // 128
COLS = GROUP * N
LAG_GATES = GROUP
LAG_FINAL = 2 * GROUP + 1
LAG_STORE = LAG_FINAL + 1
STEPS = GRAPHS + LAG_STORE
BODY = 2 * GROUP
FIRST = 4 * GROUP
ROUNDS = 5
LAST = FIRST + ROUNDS * BODY


def gnn_kernel(nc, x, adj, wdT, wgT, bd, b_r, b_z, b_n, gamma, beta, out):
    f32, f32r, bf16, i32 = mybir.dt.float32, mybir.dt.float32r, mybir.dt.bfloat16, mybir.dt.int32
    ALU, ACT = mybir.AluOpType, mybir.ActivationFunctionType

    x_groups = x.rearrange("(k g) n h -> k n g h", g=GROUP)
    adj_groups = adj.rearrange("(k g) m n -> k m g n", g=GROUP)

    ctx = ExitStack()
    with ctx:
        def sb(name, shape, dt=f32):
            return ctx.enter_context(nc.sbuf_tensor(name, shape, dt))

        def bank(name):
            return ctx.enter_context(nc.psum_tensor(name, [128, 512], f32))

        def sem(name):
            return ctx.enter_context(nc.semaphore(name))

        wd_f = sb("wd_f", [128, HC, D * H])
        wd_hi = sb("wd_hi", [128, HC, D * H], f32r)
        wd_lo = sb("wd_lo", [128, HC, D * H], f32r)
        wg_f = sb("wg_f", [128, HC, 6 * H])
        wg_hi = sb("wg_hi", [128, HC, 6 * H], f32r)
        wg_lo = sb("wg_lo", [128, HC, 6 * H], f32r)
        ident = sb("ident", [128, 128])
        ones_bf = sb("ones_bf", [128, 1], bf16)
        labels = sb("labels", [128, D, N])
        bd_rows = sb("bd_rows", [128, H])
        gamma_rows = sb("gamma_rows", [128, H])
        beta_rows = sb("beta_rows", [128, H])
        bias_in = sb("bias_in", [128, 6, HC])
        bias_r = sb("bias_r", [128, HC])
        bias_z = sb("bias_z", [128, HC])
        power = sb("power", [128, 1])
        ln_eps = sb("ln_eps", [128, 1])
        x_in = sb("x_in", [128, 2, GROUP, H])
        adj_in = sb("adj_in", [128, 2, GROUP, N], i32)
        xT_f = sb("xT_f", [128, 2, HC, COLS])
        xT_hi = sb("xT_hi", [128, 2, HC, COLS], f32r)
        xT_lo = sb("xT_lo", [128, 2, HC, COLS], f32r)
        x_keep = sb("x_keep", [128, COLS])
        masks = sb("masks", [128, 2, D, N], f32r)
        y_hi = sb("y_hi", [128, D * H], f32r)
        y_lo = sb("y_lo", [128, D * H], f32r)
        counts = sb("counts", [128, D])
        rcount = sb("rcount", [128, D])
        out_rows = sb("out_rows", [128, H])
        oT_hi = sb("oT_hi", [128, 2, HC, COLS], f32r)
        oT_lo = sb("oT_lo", [128, 2, HC, COLS], f32r)
        r_sb = sb("r_sb", [128, COLS])
        z_sb = sb("z_sb", [128, COLS])
        rn_sb = sb("rn_sb", [128, COLS])
        pre_n = sb("pre_n", [128, COLS])
        n_sb = sb("n_sb", [128, COLS])
        h_minus_n = sb("h_minus_n", [128, COLS])
        z_part = sb("z_part", [128, COLS])
        mixT = sb("mixT", [128, 2, HC, COLS])
        stats = sb("stats", [128, 6])
        mean_var = sb("mean_var", [128, 2, 2])
        var_eps = sb("var_eps", [128, 1])
        rstd = sb("rstd", [128, 2])
        centred = sb("centred", [128, 2, H])
        normed = sb("normed", [128, GROUP, H])

        y_bank = [bank("y_bank0"), bank("y_bank1")]
        p_bank = [bank("p_bank0"), bank("p_bank1")]
        rz_bank = bank("rz_bank")
        n_bank = bank("n_bank")
        in_bank = bank("in_bank")
        io_bank = bank("io_bank")

        wd_loaded = sem("wd_loaded")
        wg_loaded = sem("wg_loaded")
        vec_loaded = sem("vec_loaded")
        ident_zero = sem("ident_zero")
        const_ready = sem("const_ready")
        wd_hi_ready = sem("wd_hi_ready")
        wd_ready = sem("wd_ready")
        wg_hi_ready = sem("wg_hi_ready")
        wg_ready = sem("wg_ready")
        bias_ready = sem("bias_ready")
        in_loaded = [sem("in_loaded0"), sem("in_loaded1")]
        stored = [sem(f"stored{g}") for g in range(GROUP)]
        inT_done = sem("inT_done")
        xhi_ready = sem("xhi_ready")
        xf_ready = sem("xf_ready")
        xlo_ready = sem("xlo_ready")
        masks_ready = sem("masks_ready")
        y0_done = sem("y0_done")
        y1_done = sem("y1_done")
        yhi0_ready = sem("yhi0_ready")
        yhi1_ready = sem("yhi1_ready")
        ylo0_ready = sem("ylo0_ready")
        ylo1_ready = sem("ylo1_ready")
        p_done = sem("p_done")
        label_sum = [sem(f"label_sum{d}") for d in range(D)]
        io_done = sem("io_done")
        ohi_ready = sem("ohi_ready")
        counts_ready = sem("counts_ready")
        rcount_ready = sem("rcount_ready")
        olo_ready = sem("olo_ready")
        hid_used = sem("hid_used")
        n_done = sem("n_done")
        rz_done = sem("rz_done")
        rz_read = sem("rz_read")
        n_read = sem("n_read")
        tanh_ready = sem("tanh_ready")
        keep_ready = sem("keep_ready")
        hn_ready = sem("hn_ready")
        zp_ready = sem("zp_ready")
        mix_ready = sem("mix_ready")
        rows_done = sem("rows_done")
        stats_ready = sem("stats_ready")
        mv_ready = sem("mv_ready")
        rows_read = sem("rows_read")
        ve_ready = sem("ve_ready")
        rstd_ready = sem("rstd_ready")
        norm_ready = sem("norm_ready")

        def run_steps(eng, step):
            for i in range(FIRST):
                step(i, lambda n, k=BODY: n)
            with eng.Fori(0, ROUNDS) as rnd:
                for i in range(FIRST, FIRST + BODY):
                    step(i, lambda n, k=BODY: rnd * k + n)
            for i in range(LAST, STEPS):
                step(i, lambda n, k=BODY: n)

        def has_graph(i):
            return 0 <= i < GRAPHS

        def part_of(i):
            p = i - LAG_GATES
            return p, (p % GROUP) // 2, p % 2 == 1

        def ring(graph):
            return (graph // GROUP) % 2

        def cols(graph):
            return slice((graph % GROUP) * N, (graph % GROUP + 1) * N)

        block = ctx.enter_context(nc.Block())

        @block.sync
        def _(sp):
            def load_group(k, index):
                sp.dma_start(x_in[:, k % 2, :, :], x_groups[index]).then_inc(in_loaded[k % 2], 16)
                sp.dma_start(adj_in[:, k % 2, :, :], adj_groups[index]).then_inc(in_loaded[k % 2], 16)

            load_group(0, 0)
            for c in range(HC):
                sp.dma_start(wd_f[:, c, :], wdT[:, c, :]).then_inc(wd_loaded, 16)
            for t, src in enumerate((bd, gamma, beta)):
                dst = (bd_rows, gamma_rows, beta_rows)[t]
                sp.dma_start(dst[:, :], src.partition_broadcast(128)).then_inc(vec_loaded, 16)
            for t, src in enumerate((b_r, b_z, b_n)):
                sp.dma_start(bias_in[:, 2 * t:2 * t + 2, :], src).then_inc(vec_loaded, 16)
            for c in range(HC):
                sp.dma_start(wg_f[:, c, :], wgT[:, c, :]).then_inc(wg_loaded, 16)

            def step(i, up):
                k = i // GROUP
                if i % GROUP == 0 and (k + 1) * GROUP < GRAPHS:
                    if k >= 1:
                        sp.wait_ge(inT_done, up(k * GROUP))
                    load_group(k + 1, up(k + 1, 2))
                j = i - LAG_STORE
                if has_graph(j):
                    sp.wait_ge(norm_ready, up(j + 1))
                    sp.dma_start(out[up(j)], normed[:, j % GROUP, :]).then_inc(stored[j % GROUP], 16)

            run_steps(sp, step)
            for g in range(GROUP):
                sp.wait_ge(stored[g], 16 * GRAPHS // GROUP)

        @block.tensor
        def _(pe):
            def transpose_inputs(i, up):
                if i % GROUP == 0:
                    pe.wait_ge(in_loaded[ring(i)], up(32 * (i // BODY + 1), 32))
                slot = ring(i)
                for c in range(HC):
                    nc.tensor.transpose(in_bank[:, c * 128:(c + 1) * 128],
                                        x_in[:, slot, i % GROUP, c * 128:(c + 1) * 128], ident[:, :])
                nc.tensor.transpose(in_bank[:, H:H + N], adj_in[:, slot, i % GROUP, :].bitcast(f32),
                                    ident[:, :]).then_inc(inT_done, 1)

            def project(i, up):
                for b in range(2):
                    if i >= 1:
                        pe.wait_ge((ylo0_ready, ylo1_ready)[b], up(i))
                    o = slice(b * 512, (b + 1) * 512)
                    terms = [(xT_hi, wd_hi), (xT_hi, wd_lo), (xT_lo, wd_hi)]
                    for c in range(HC):
                        for t, (xt, w) in enumerate(terms):
                            last = nc.tensor.matmul(y_bank[b][:, :], xt[:, ring(i), c, cols(i)], w[:, c, o],
                                                    start=(c == 0 and t == 0), stop=(c == HC - 1 and t == 2))
                    last.then_inc((y0_done, y1_done)[b], 1)

            def gate_terms(bank_, gate, o, w_in, hi, lo, slot, first, final):
                at = slice(gate * H + o * 128, gate * H + (o + 1) * 128)
                for c in range(HC):
                    for t, (w, m) in enumerate([(wg_hi, hi), (wg_hi, lo), (wg_lo, hi)]):
                        last = nc.tensor.matmul(bank_[:, :], w[:, c, at], m[:, slot, c, :],
                                                start=(first and c == 0 and t == 0),
                                                stop=(final and c == HC - 1 and t == 2))
                return last

            pe.wait_ge(const_ready, 1)
            transpose_inputs(0, lambda n, k=0: n)

            def step(i, up):
                if has_graph(i):
                    if i == 0:
                        pe.wait_ge(wd_ready, 1)
                    pe.wait_ge(xlo_ready, up(i + 1))
                    project(i, up)
                if i <= GRAPHS:
                    if i - LAG_STORE >= 0:
                        pe.wait_ge(rows_read, up(i - LAG_STORE + 1))
                    if has_graph(i):
                        pe.wait_ge(masks_ready, up(i + 1))
                        halves = masks[:, i % 2, :, :].bitcast(bf16).rearrange("n d (m t) -> n d m t", t=2)
                        for d in range(D):
                            last = nc.tensor.matmul(io_bank[:, H + d:H + d + 1], halves[:, d, :, 1],
                                                    ones_bf[:, :], start=True, stop=True)
                    if has_graph(i - 1):
                        pe.wait_ge(label_sum[D - 1], up(i))
                        for c in range(HC):
                            last = nc.tensor.transpose(io_bank[:, c * 128:(c + 1) * 128],
                                                       out_rows[:, c * 128:(c + 1) * 128], ident[:, :])
                    last.then_inc(io_done, 1)
                if has_graph(i + 1):
                    transpose_inputs(i + 1, up)
                p, o, is_zn = part_of(i)
                if has_graph(p):
                    slot = ring(p)
                    if p == 0:
                        pe.wait_ge(wg_ready, 1)
                    else:
                        pe.wait_ge(rz_read, up(p))
                    last = gate_terms(rz_bank, 4 if is_zn else 3, o, None, xT_hi, xT_lo, slot, True, False)
                    if is_zn:
                        last.then_inc(hid_used, 1)
                    if p:
                        pe.wait_ge(n_read, up(p))
                    if is_zn:
                        last = gate_terms(n_bank, 2, o, None, oT_hi, oT_lo, slot, True, True)
                        last.then_inc(n_done, 1)
                    else:
                        last = gate_terms(n_bank, 5, o, None, xT_hi, xT_lo, slot, True, True)
                        last.then_inc(n_done, 1)
                        last = None
                j = i - LAG_FINAL
                if has_graph(j):
                    if i <= GRAPHS:
                        pe.wait_ge(olo_ready, up(i))
                    else:
                        pe.wait_ge(rows_read, up(j))
                    if j % GROUP == 0:
                        pe.wait_ge(mix_ready, up(2 * (j // GROUP + 1), 4))
                    for c in range(HC):
                        last = nc.tensor.transpose(io_bank[:, c * 128:(c + 1) * 128],
                                                   mixT[:, ring(j), c, cols(j)], ident[:, :])
                    last.then_inc(rows_done, 1)
                if has_graph(p):
                    if p % GROUP == 0:
                        pe.wait_ge(olo_ready, up(p + GROUP))
                    gate_terms(rz_bank, 1 if is_zn else 0, o, None, oT_hi, oT_lo, slot, False, True)\
                        .then_inc(rz_done, 1)
                if has_graph(i):
                    pe.wait_ge(ylo1_ready, up(i + 1))
                    for d in range(D):
                        for y in (y_hi, y_lo):
                            last = nc.tensor.matmul(p_bank[d // 2][:, (d % 2) * H:(d % 2 + 1) * H],
                                                    masks[:, i % 2, d, :], y[:, d * H:(d + 1) * H],
                                                    start=(y is y_hi), stop=(y is y_lo))
                    last.then_inc(p_done, 1)

            run_steps(pe, step)

        @block.scalar
        def _(act):
            def split_inputs(i, up):
                act.wait_ge(inT_done, up(i + 1))
                src = in_bank[:, 0:H].rearrange("p (c n) -> p c n", c=HC)
                if i % GROUP == 0 and i >= BODY:
                    act.wait_ge(hid_used, up(2 * (i // GROUP - 1), 4))
                nc.scalar.activation(xT_hi[:, ring(i), :, cols(i)], src, ACT.Copy).then_inc(xhi_ready, 1)
                if i % GROUP == 0 and i >= BODY:
                    act.wait_ge(hn_ready, up(2 * (i // GROUP - 2) + 1, 4))
                    act.wait_ge(keep_ready, up(i // GROUP - 1, 2))
                nc.scalar.activation(xT_f[:, ring(i), :, cols(i)], src, ACT.Copy).then_inc(xf_ready, 1)

            act.wait_ge(wd_loaded, 16 * HC)
            nc.scalar.activation(wd_hi[:, :, :], wd_f[:, :, :], ACT.Copy).then_inc(wd_hi_ready, 1)
            split_inputs(0, lambda n, k=0: n)

            def step(i, up):
                p, o, is_zn = part_of(i - 1)
                if has_graph(p):
                    if p == 0:
                        act.wait_ge(bias_ready, 2)
                    act.wait_ge(rz_done, up(p + 1))
                    if p >= 2:
                        if is_zn:
                            act.wait_ge(mix_ready, up((p - 1) // 2, 4))
                        else:
                            act.wait_ge(n_read, up(p - 1))
                    dst, b = (z_sb, bias_z) if is_zn else (r_sb, bias_r)
                    nc.scalar.activation(dst[:, :], rz_bank[:, :], ACT.Sigmoid, bias=b[:, o:o + 1])\
                        .then_inc(rz_read, 1)
                    if is_zn:
                        act.wait_ge(n_read, up(p + 1))
                        nc.scalar.activation(n_sb[:, :], pre_n[:, :], ACT.Tanh, bias=bias_in[:, 4, o:o + 1])\
                            .then_inc(tanh_ready, 1)
                if has_graph(i):
                    for b in range(2):
                        act.wait_ge((y0_done, y1_done)[b], up(i + 1))
                        nc.scalar.activation(y_hi[:, b * 512:(b + 1) * 512], y_bank[b][:, :], ACT.Copy)\
                            .then_inc((yhi0_ready, yhi1_ready)[b], 1)
                if has_graph(i - 1):
                    act.wait_ge(io_done, up(i + 1))
                    src = io_bank[:, 0:H].rearrange("p (c n) -> p c n", c=HC)
                    nc.scalar.activation(oT_hi[:, ring(i - 1), :, cols(i - 1)], src, ACT.Relu)\
                        .then_inc(ohi_ready, 1)
                if i == 0:
                    act.wait_ge(wg_loaded, 16 * HC)
                    for c in range(HC):
                        nc.scalar.activation(wg_hi[:, c, :], wg_f[:, c, :], ACT.Copy).then_inc(wg_hi_ready, 1)
                if has_graph(i + 1):
                    split_inputs(i + 1, up)
                p, o, is_zn = part_of(i)
                if has_graph(p) and p % GROUP == 2:
                    if p >= GROUP:
                        act.wait_ge(hn_ready, up(2 * (p // GROUP), 4))
                    nc.scalar.activation(x_keep[:, :], xT_f[:, ring(p), 1, :], ACT.Copy)\
                        .then_inc(keep_ready, 1)

            run_steps(act, step)

        @block.vector
        def _(dve):
            def split_inputs(i, up):
                dve.wait_ge(xf_ready, up(i + 1))
                nc.vector.tensor_tensor(xT_lo[:, ring(i), :, cols(i)], xT_f[:, ring(i), :, cols(i)],
                                        xT_hi[:, ring(i), :, cols(i)].bitcast(f32), ALU.subtract)\
                    .then_inc(xlo_ready, 1)
                if i >= 2:
                    dve.wait_ge(p_done, up(i - 1))
                adjT = in_bank[:, H:H + N].bitcast(i32).unsqueeze(1).broadcast_to([128, D, N])
                nc.vector.tensor_tensor(masks[:, i % 2, :, :], adjT, labels[:, :, :], ALU.is_equal)\
                    .then_inc(masks_ready, 1)

            for d in range(D):
                last = nc.vector.memset(labels[:, d, :], float(d + 1))
            last.then_inc(bias_ready, 1)
            dve.wait_ge(bias_ready, 1)
            split_inputs(0, lambda n, k=0: n)
            dve.wait_ge(wd_hi_ready, 1)
            nc.vector.tensor_tensor(wd_lo[:, :, :], wd_f[:, :, :], wd_hi[:, :, :].bitcast(f32), ALU.subtract)\
                .then_inc(wd_ready, 1)
            dve.wait_ge(vec_loaded, 16 * 6)
            nc.vector.tensor_tensor(bias_r[:, :], bias_in[:, 0, :], bias_in[:, 1, :], ALU.add)
            nc.vector.tensor_tensor(bias_z[:, :], bias_in[:, 2, :], bias_in[:, 3, :], ALU.add)\
                .then_inc(bias_ready, 1)

            def step(i, up):
                p, o, is_zn = part_of(i - 1)
                if has_graph(p):
                    if not is_zn:
                        dve.wait_ge(rz_read, up(p + 1))
                        nc.vector.scalar_tensor_tensor(rn_sb[:, :], n_bank[:, :], bias_in[:, 5, o:o + 1],
                                                       r_sb[:, :], ALU.add, ALU.mult).then_inc(n_read, 1)
                    else:
                        dve.wait_ge(n_done, up(p + 1))
                        dve.wait_ge(n_read, up(p))
                        if p >= 2:
                            dve.wait_ge(tanh_ready, up((p - 1) // 2, 4))
                        nc.vector.tensor_tensor(pre_n[:, :], n_bank[:, :], rn_sb[:, :], ALU.add)\
                            .then_inc(n_read, 1)
                if has_graph(i - 1):
                    dve.wait_ge(p_done, up(i))
                    for d in range(D):
                        dve.wait_ge(label_sum[d - 1] if d else rcount_ready, up(i))
                        nc.vector.scalar_tensor_tensor(
                            out_rows[:, :], p_bank[d // 2][:, (d % 2) * H:(d % 2 + 1) * H], rcount[:, d:d + 1],
                            out_rows[:, :] if d else bd_rows[:, :], ALU.mult, ALU.add).then_inc(label_sum[d], 1)
                j = i - LAG_STORE
                if has_graph(j):
                    dve.wait_ge(rstd_ready, up(j + 1))
                    dve.wait_ge(rows_read, up(j + 1))
                    if j >= GROUP:
                        dve.wait_ge(stored[j % GROUP], up(16 * (j // GROUP), 32))
                    nc.vector.scalar_tensor_tensor(normed[:, j % GROUP, :], centred[:, j % 2, :],
                                                   rstd[:, j % 2:j % 2 + 1], beta_rows[:, :],
                                                   ALU.mult, ALU.add).then_inc(norm_ready, 1)
                if has_graph(i):
                    for b in range(2):
                        dve.wait_ge((yhi0_ready, yhi1_ready)[b], up(i + 1))
                        at = slice(b * 512, (b + 1) * 512)
                        nc.vector.tensor_tensor(y_lo[:, at], y_bank[b][:, :], y_hi[:, at].bitcast(f32),
                                                ALU.subtract).then_inc((ylo0_ready, ylo1_ready)[b], 1)
                if i <= GRAPHS:
                    if i == 0:
                        dve.wait_ge(io_done, 1)
                    else:
                        dve.wait_ge(ohi_ready, up(i))
                if has_graph(i):
                    nc.vector.tensor_scalar(counts[:, :], io_bank[:, H:H + D], EPS, None, ALU.add)\
                        .then_inc(counts_ready, 1)
                if has_graph(i - 1):
                    src = io_bank[:, 0:H].rearrange("p (c n) -> p c n", c=HC)
                    nc.vector.scalar_tensor_tensor(oT_lo[:, ring(i - 1), :, cols(i - 1)], src, 0.0,
                                                   oT_hi[:, ring(i - 1), :, cols(i - 1)].bitcast(f32),
                                                   ALU.max, ALU.subtract).then_inc(olo_ready, 1)
                if has_graph(i):
                    dve.wait_ge(counts_ready, up(i + 1))
                    nc.vector.reciprocal(rcount[:, :], counts[:, :]).then_inc(rcount_ready, 1)
                if i == 0:
                    for c in range(HC):
                        dve.wait_ge(wg_hi_ready, c + 1)
                        last = nc.vector.tensor_tensor(wg_lo[:, c, :], wg_f[:, c, :], wg_hi[:, c, :].bitcast(f32),
                                                       ALU.subtract)
                    last.then_inc(wg_ready, 1)
                if has_graph(i + 1):
                    split_inputs(i + 1, up)
                if has_graph(p) and is_zn:
                    dve.wait_ge(hn_ready, up((p + 1) // 2, 4))
                    dve.wait_ge(rz_read, up(p + 1))
                    nc.vector.tensor_tensor(z_part[:, :], z_sb[:, :], h_minus_n[:, :], ALU.mult)\
                        .then_inc(zp_ready, 1)
                j = i - LAG_FINAL
                if has_graph(j):
                    dve.wait_ge(rows_done, up(j + 1))
                    nc.vector.bn_stats(stats[:, :], io_bank[:, 0:H]).then_inc(stats_ready, 1)
                if has_graph(p) and is_zn:
                    dve.wait_ge(zp_ready, up((p + 1) // 2, 4))
                    nc.vector.tensor_tensor(mixT[:, ring(p), o, :], z_part[:, :], n_sb[:, :], ALU.add)\
                        .then_inc(mix_ready, 1)
                if has_graph(j):
                    dve.wait_ge(vec_loaded, 16 * 6)
                    dve.wait_ge(stats_ready, up(j + 1))
                    nc.vector.bn_aggr(mean_var[:, j % 2, :], stats[:, :]).then_inc(mv_ready, 1)
                    dve.wait_ge(mv_ready, up(j + 1))
                    nc.vector.scalar_tensor_tensor(centred[:, j % 2, :], io_bank[:, 0:H],
                                                   mean_var[:, j % 2, 0:1], gamma_rows[:, :],
                                                   ALU.subtract, ALU.mult).then_inc(rows_read, 1)

            run_steps(dve, step)

        @block.gpsimd
        def _(pool):
            nc.gpsimd.memset(ones_bf[:, :], 1.0)
            nc.gpsimd.memset(ln_eps[:, :], LN_EPS)
            nc.gpsimd.memset(power[:, :], -0.5).then_inc(ident_zero, 1)
            nc.gpsimd.memset(ident[:, :], 0.0).then_inc(ident_zero, 1)
            pool.wait_ge(ident_zero, 2)
            nc.gpsimd.affine_select(out=ident[:, :], in_=ident[:, :], compare_op=ALU.not_equal, fill=1.0,
                                    base=0, pattern=[[-1, 128]], channel_multiplier=1).then_inc(const_ready, 1)

            def step(i, up):
                p, o, is_zn = part_of(i - 1)
                if has_graph(p) and is_zn:
                    half = (p + 1) // 2
                    pool.wait_ge(tanh_ready, up(half, 4))
                    if half > 1:
                        pool.wait_ge(zp_ready, up(half - 1, 4))
                    if o:
                        pool.wait_ge(keep_ready, up(p // GROUP + 1, 2))
                    h = x_keep[:, :] if o else xT_f[:, ring(p), 0, :]
                    nc.gpsimd.tensor_tensor(h_minus_n[:, :], h, n_sb[:, :], ALU.subtract).then_inc(hn_ready, 1)
                j = i - LAG_FINAL
                if has_graph(j):
                    pool.wait_ge(mv_ready, up(j + 1))
                    nc.gpsimd.tensor_tensor(var_eps[:, :], mean_var[:, j % 2, 1:2], ln_eps[:, :], ALU.add)\
                        .then_inc(ve_ready, 1)
                    pool.wait_ge(ve_ready, up(j + 1))
                    nc.gpsimd.tensor_tensor(rstd[:, j % 2:j % 2 + 1], var_eps[:, :], power[:, :], ALU.pow)\
                        .then_inc(rstd_ready, 1)

            run_steps(pool, step)


def kernel(x, adj, L0_gnn_Wd, L0_gnn_bd, L0_gnn_Wri, L0_gnn_bri, L0_gnn_Wrh, L0_gnn_brh, L0_gnn_Wzi, L0_gnn_bzi,
           L0_gnn_Wzh, L0_gnn_bzh, L0_gnn_Wni, L0_gnn_bni, L0_gnn_Wnh, L0_gnn_bnh, L0_gnn_gamma, L0_gnn_beta):
    import numpy as np
    import concourse.bacc as bacc
    from concourse.bass_utils import run_bass_kernel_spmd

    def chunked(w):
        w = np.asarray(w)
        return w.T.reshape(HC, 128, w.shape[0]).transpose(1, 0, 2)

    def column(b):
        return np.asarray(b).reshape(HC, 128).T

    def pair(a, b):
        return np.ascontiguousarray(np.stack([column(a), column(b)], axis=1))

    wd = np.asarray(L0_gnn_Wd).reshape(H, D, H)
    wdT = np.concatenate([chunked(wd[:, d, :]) for d in range(D)], axis=2)
    wgT = np.concatenate([chunked(w) for w in (L0_gnn_Wri, L0_gnn_Wzi, L0_gnn_Wni,
                                               L0_gnn_Wrh, L0_gnn_Wzh, L0_gnn_Wnh)], axis=2)
    arrays = {
        "x": np.ascontiguousarray(x), "adj": np.ascontiguousarray(adj),
        "wdT": np.ascontiguousarray(wdT), "wgT": np.ascontiguousarray(wgT),
        "bd": np.ascontiguousarray(L0_gnn_bd),
        "b_r": pair(L0_gnn_bri, L0_gnn_brh), "b_z": pair(L0_gnn_bzi, L0_gnn_bzh),
        "b_n": pair(L0_gnn_bni, L0_gnn_bnh),
        "gamma": np.ascontiguousarray(L0_gnn_gamma), "beta": np.ascontiguousarray(L0_gnn_beta),
    }
    nc = bacc.Bacc("TRN2", target_bir_lowering=False, num_devices=1)
    args = [nc.dram_tensor(f"in_{n}", a.shape, mybir.dt.from_np(a.dtype), kind="ExternalInput").ap()
            for n, a in arrays.items()]
    args.append(nc.dram_tensor("out", (GRAPHS, N, H), mybir.dt.float32, kind="ExternalOutput").ap())
    gnn_kernel(nc, *args)
    res = run_bass_kernel_spmd(nc, [{f"in_{n}": a for n, a in arrays.items()}], core_ids=[0])
    return res.results[0]["out"]
```

```python
import concourse.bass as bass
from concourse import mybir
from contextlib import ExitStack

GRAPHS, N, H, D = 64, 128, 256, 4
EPS, LN_EPS = 1e-8, 1e-5
GROUP = 4
HC = H // 128
COLS = GROUP * N
LAG_GATES = GROUP
LAG_FINAL = 2 * GROUP + 1
LAG_STORE = LAG_FINAL + 1
STEPS = GRAPHS + LAG_STORE
BODY = 2 * GROUP
FIRST = 4 * GROUP
ROUNDS = 5
TAIL = GRAPHS - GROUP
WG_PIECES = 3
LAST = FIRST + ROUNDS * BODY


def gnn_kernel(nc, xT, adjT, wdT, wgT, bd, b_r, b_z, b_n, gamma, beta, out):
    f32, f32r, bf16, i32 = mybir.dt.float32, mybir.dt.float32r, mybir.dt.bfloat16, mybir.dt.int32
    ALU, ACT = mybir.AluOpType, mybir.ActivationFunctionType

    ctx = ExitStack()
    with ctx:
        def sb(name, shape, dt=f32):
            return ctx.enter_context(nc.sbuf_tensor(name, shape, dt))

        def bank(name):
            return ctx.enter_context(nc.psum_tensor(name, [128, 512], f32))

        def sem(name):
            return ctx.enter_context(nc.semaphore(name))

        wd_f = sb("wd_f", [128, HC, D * H])
        wd_hi = sb("wd_hi", [128, HC, D * H], f32r)
        wd_lo = sb("wd_lo", [128, HC, D * H], f32r)
        wg_f = sb("wg_f", [128, HC, 6 * H])
        wg_hi = sb("wg_hi", [128, HC, 6 * H], f32r)
        wg_lo = sb("wg_lo", [128, HC, 6 * H], f32r)
        ident = sb("ident", [128, 128])
        ones_bf = sb("ones_bf", [128, 1], bf16)
        labels = sb("labels", [128, D, N])
        bd_rows = sb("bd_rows", [128, H])
        gamma_rows = sb("gamma_rows", [128, H])
        beta_rows = sb("beta_rows", [128, H])
        bias_in = sb("bias_in", [128, 6, HC])
        bias_r = sb("bias_r", [128, HC])
        bias_z = sb("bias_z", [128, HC])
        power = sb("power", [128, 1])
        ln_eps = sb("ln_eps", [128, 1])
        xT_f = sb("xT_f", [128, 2, HC, COLS])
        adjT_in = sb("adjT_in", [128, 2, COLS], i32)
        xT_hi = sb("xT_hi", [128, 2, HC, COLS], f32r)
        xT_lo = sb("xT_lo", [128, 2, HC, COLS], f32r)
        x_keep = sb("x_keep", [128, HC, COLS])
        masks = sb("masks", [128, 2, D, N], f32r)
        y_hi = sb("y_hi", [128, D * H], f32r)
        y_lo = sb("y_lo", [128, D * H], f32r)
        counts = sb("counts", [128, D])
        rcount = sb("rcount", [128, D])
        out_rows = sb("out_rows", [128, H])
        oT_hi = sb("oT_hi", [128, 2, HC, COLS], f32r)
        oT_lo = sb("oT_lo", [128, 2, HC, COLS], f32r)
        r_sb = sb("r_sb", [128, COLS])
        z_sb = sb("z_sb", [128, COLS])
        rn_sb = sb("rn_sb", [128, COLS])
        pre_n = sb("pre_n", [128, COLS])
        n_sb = sb("n_sb", [128, COLS])
        h_minus_n = sb("h_minus_n", [128, COLS])
        z_part = sb("z_part", [128, COLS])
        mixT = sb("mixT", [128, 2, HC, COLS])
        stats = sb("stats", [128, 6])
        mean_var = sb("mean_var", [128, 2, 2])
        var_eps = sb("var_eps", [128, 1])
        rstd = sb("rstd", [128, 2])
        centred = sb("centred", [128, 2, H])
        normed = sb("normed", [128, GROUP, H])

        y_bank = [bank("y_bank0"), bank("y_bank1")]
        p_bank = [bank("p_bank0"), bank("p_bank1")]
        rz_bank = bank("rz_bank")
        n_bank = bank("n_bank")
        out_bank = bank("out_bank")
        row_bank = bank("row_bank")

        wd_loaded = [sem(f"wd_loaded{t}") for t in range(2 * HC)]
        wg_loaded = [sem(f"wg_loaded{c}") for c in range(HC)]
        vec_loaded = sem("vec_loaded")
        ident_zero = sem("ident_zero")
        const_ready = sem("const_ready")
        labels_ready = sem("labels_ready")
        wd_hi_ready = sem("wd_hi_ready")
        wd_ready = sem("wd_ready")
        wg_hi_ready = sem("wg_hi_ready")
        wg_ready = sem("wg_ready")
        bias_ready = sem("bias_ready")
        first_loaded = sem("first_loaded")
        in_loaded = [sem("in_loaded0"), sem("in_loaded1")]
        stored = [sem(f"stored{g}") for g in range(GROUP)]
        xhi_ready = sem("xhi_ready")
        xlo_ready = sem("xlo_ready")
        masks_ready = sem("masks_ready")
        y0_done = sem("y0_done")
        y1_done = sem("y1_done")
        yhi0_ready = sem("yhi0_ready")
        yhi1_ready = sem("yhi1_ready")
        ylo0_ready = sem("ylo0_ready")
        ylo1_ready = sem("ylo1_ready")
        p_done = sem("p_done")
        label_sum = [sem(f"label_sum{d}") for d in range(D)]
        out_done = sem("out_done")
        ohi_ready = sem("ohi_ready")
        counts_ready = sem("counts_ready")
        rcount_ready = sem("rcount_ready")
        olo_ready = sem("olo_ready")
        hid_used = sem("hid_used")
        n_done = sem("n_done")
        rz_done = sem("rz_done")
        rz_read = sem("rz_read")
        n_read = sem("n_read")
        tanh_ready = sem("tanh_ready")
        keep_ready = sem("keep_ready")
        hn_ready = sem("hn_ready")
        zp_ready = sem("zp_ready")
        mix_ready = sem("mix_ready")
        rows_done = sem("rows_done")
        stats_ready = sem("stats_ready")
        mv_ready = sem("mv_ready")
        rows_read = sem("rows_read")
        ve_ready = sem("ve_ready")
        rstd_ready = sem("rstd_ready")
        norm_ready = sem("norm_ready")

        def run_steps(eng, step):
            for i in range(FIRST):
                step(i, lambda n, k=BODY: n)
            with eng.Fori(0, ROUNDS) as rnd:
                for i in range(FIRST, FIRST + BODY):
                    step(i, lambda n, k=BODY: rnd * k + n)
            for i in range(LAST, STEPS):
                step(i, lambda n, k=BODY: n)

        def has_graph(i):
            return 0 <= i < GRAPHS

        def part_of(i):
            p = i - LAG_GATES
            return p, (p % GROUP) // 2, p % 2 == 1

        def part_banks(p):
            return (y_bank[0], y_bank[1]) if p > TAIL and (p - TAIL) % 2 else (rz_bank, n_bank)

        def rows_bank(j):
            return (row_bank, p_bank[0], p_bank[1], out_bank)[j - TAIL] if j > TAIL else row_bank

        def ring(graph):
            return (graph // GROUP) % 2

        def cols(graph):
            return slice((graph % GROUP) * N, (graph % GROUP + 1) * N)

        block = ctx.enter_context(nc.Block())

        def load_wd(eng, b, c):
            at = slice(b * 512, (b + 1) * 512)
            eng.dma_start(wd_f[:, c, at], wdT[:, c, at]).then_inc(wd_loaded[b * HC + c], 16)

        @block.sync
        def _(sp):
            def load_group(k, index):
                sp.dma_start(xT_f[:, k % 2, :, :], xT[index]).then_inc(in_loaded[k % 2], 16)
                sp.dma_start(adjT_in[:, k % 2, :], adjT[index]).then_inc(in_loaded[k % 2], 16)

            sp.dma_start(xT_f[:, 0, :, 0:N], xT[0, :, :, 0:N]).then_inc(first_loaded, 16)
            load_wd(sp, 0, 0)
            load_wd(sp, 1, 0)
            sp.dma_start(xT_f[:, 0, :, N:COLS], xT[0, :, :, N:COLS]).then_inc(in_loaded[0], 16)
            sp.dma_start(adjT_in[:, 0, N:COLS], adjT[0, :, N:COLS]).then_inc(in_loaded[0], 16)
            for t, src in enumerate((bd, gamma, beta)):
                dst = (bd_rows, gamma_rows, beta_rows)[t]
                sp.dma_start(dst[:, :], src.partition_broadcast(128)).then_inc(vec_loaded, 16)
            for t, src in enumerate((b_r, b_z, b_n)):
                sp.dma_start(bias_in[:, 2 * t:2 * t + 2, :], src).then_inc(vec_loaded, 16)
            for c in range(HC):
                sp.dma_start(wg_f[:, c, :], wgT[:, c, :]).then_inc(wg_loaded[c], 16)
            load_group(1, 1)

            def step(i, up):
                k = i // GROUP
                if i % GROUP == 1 and k >= 1 and (k + 1) * GROUP < GRAPHS:
                    sp.wait_ge(keep_ready, up(k, 2))
                    load_group(k + 1, up(k + 1, 2))
                j = i - LAG_STORE
                if has_graph(j):
                    sp.wait_ge(norm_ready, up(j + 1))
                    sp.dma_start(out[up(j)], normed[:, j % GROUP, :]).then_inc(stored[j % GROUP], 16)

            run_steps(sp, step)
            for g in range(GROUP):
                sp.wait_ge(stored[g], 16 * GRAPHS // GROUP)

        @block.tensor
        def _(pe):
            def project(i, up):
                for b in range(2):
                    if i >= 1:
                        pe.wait_ge((ylo0_ready, ylo1_ready)[b], up(i))
                    o = slice(b * 512, (b + 1) * 512)
                    terms = [(xT_hi, wd_hi), (xT_hi, wd_lo), (xT_lo, wd_hi)]
                    for c in range(HC):
                        if i == 0:
                            pe.wait_ge(wd_ready, b * HC + c + 1)
                        for t, (xt, w) in enumerate(terms):
                            last = nc.tensor.matmul(y_bank[b][:, :], xt[:, ring(i), c, cols(i)], w[:, c, o],
                                                    start=(c == 0 and t == 0), stop=(c == HC - 1 and t == 2))
                    last.then_inc((y0_done, y1_done)[b], 1)

            def gate_terms(bank_, gate, o, hi, lo, slot, first, final):
                at = slice(gate * H + o * 128, gate * H + (o + 1) * 128)
                for c in range(HC):
                    for t, (w, m) in enumerate([(wg_hi, hi), (wg_hi, lo), (wg_lo, hi)]):
                        last = nc.tensor.matmul(bank_[:, :], w[:, c, at], m[:, slot, c, :],
                                                start=(first and c == 0 and t == 0),
                                                stop=(final and c == HC - 1 and t == 2))
                return last

            def out_and_counts(i, up):
                if i >= 1:
                    pe.wait_ge(rcount_ready, up(i))
                if i >= 2:
                    pe.wait_ge(olo_ready, up(i - 1))
                if has_graph(i):
                    pe.wait_ge(masks_ready, up(i + 1))
                    halves = masks[:, i % 2, :, :].bitcast(bf16).rearrange("n d (m t) -> n d m t", t=2)
                    for d in range(D):
                        last = nc.tensor.matmul(out_bank[:, H + d:H + d + 1], halves[:, d, :, 1],
                                                ones_bf[:, :], start=True, stop=True)
                if has_graph(i - 1):
                    pe.wait_ge(label_sum[D - 1], up(i))
                    for c in range(HC):
                        last = nc.tensor.transpose(out_bank[:, c * 128:(c + 1) * 128],
                                                   out_rows[:, c * 128:(c + 1) * 128], ident[:, :])
                last.then_inc(out_done, 1)

            pe.wait_ge(const_ready, 1)

            def step(i, up):
                p, o, is_zn = part_of(i)
                if has_graph(i):
                    pe.wait_ge(xlo_ready, up(i + 1))
                    project(i, up)
                if has_graph(p):
                    slot = ring(p)
                    rz, n_part = part_banks(p)
                    if p == 0:
                        for c in range(HC * WG_PIECES):
                            pe.wait_ge(wg_ready, c + 1)
                    else:
                        pe.wait_ge(rz_read, up(p if p <= TAIL else p - 1))
                    last = gate_terms(rz, 4 if is_zn else 3, o, xT_hi, xT_lo, slot, True, False)
                    if is_zn:
                        last.then_inc(hid_used, 1)
                if i <= GRAPHS:
                    out_and_counts(i, up)
                if has_graph(p):
                    if p:
                        pe.wait_ge(n_read, up(p if p <= TAIL else p - 1))
                    if is_zn:
                        last = gate_terms(n_part, 2, o, oT_hi, oT_lo, slot, True, True)
                    else:
                        last = gate_terms(n_part, 5, o, xT_hi, xT_lo, slot, True, True)
                    last.then_inc(n_done, 1)
                j = i - LAG_FINAL
                if has_graph(j):
                    if 1 <= j <= TAIL:
                        pe.wait_ge(rows_read, up(j))
                    if j % GROUP == 0:
                        pe.wait_ge(mix_ready, up(2 * (j // GROUP + 1), 4))
                    for c in range(HC):
                        last = nc.tensor.transpose(rows_bank(j)[:, c * 128:(c + 1) * 128],
                                                   mixT[:, ring(j), c, cols(j)], ident[:, :])
                    last.then_inc(rows_done, 1)
                if has_graph(p):
                    if p % GROUP == 0:
                        pe.wait_ge(olo_ready, up(p + GROUP))
                    gate_terms(rz, 1 if is_zn else 0, o, oT_hi, oT_lo, slot, False, True).then_inc(rz_done, 1)
                if has_graph(i):
                    for d in range(D):
                        if d % 2 == 0:
                            pe.wait_ge((ylo0_ready, ylo1_ready)[d // 2], up(i + 1))
                        for y in (y_hi, y_lo):
                            last = nc.tensor.matmul(p_bank[d // 2][:, (d % 2) * H:(d % 2 + 1) * H],
                                                    masks[:, i % 2, d, :], y[:, d * H:(d + 1) * H],
                                                    start=(y is y_hi), stop=(y is y_lo))
                    last.then_inc(p_done, 1)

            run_steps(pe, step)

        @block.scalar
        def _(act):
            def split_inputs(i, up):
                if i == 0:
                    act.wait_ge(first_loaded, 32)
                elif i == 1 or i % GROUP == 0:
                    act.wait_ge(in_loaded[ring(i)], up(32 * (i // BODY + 1), 32))
                if i % GROUP == 0 and i >= BODY:
                    act.wait_ge(hid_used, up(2 * (i // GROUP - 1), 4))
                nc.scalar.activation(xT_hi[:, ring(i), :, cols(i)], xT_f[:, ring(i), :, cols(i)], ACT.Copy)\
                    .then_inc(xhi_ready, 1)

            act.dma_start(adjT_in[:, 0, 0:N], adjT[0, :, 0:N]).then_inc(first_loaded, 16)
            load_wd(act, 0, 1)
            load_wd(act, 1, 1)
            split_inputs(0, lambda n, k=0: n)
            for b in range(2):
                for c in range(HC):
                    act.wait_ge(wd_loaded[b * HC + c], 16)
                    at = slice(b * 512, (b + 1) * 512)
                    nc.scalar.activation(wd_hi[:, c, at], wd_f[:, c, at], ACT.Copy).then_inc(wd_hi_ready, 1)

            def step(i, up):
                p, o, is_zn = part_of(i - 1)
                if has_graph(p):
                    rz, n_part = part_banks(p)
                    if p == 0:
                        act.wait_ge(bias_ready, 2)
                    if p >= 2:
                        if is_zn:
                            act.wait_ge(mix_ready, up((p - 1) // 2, 4))
                        else:
                            act.wait_ge(n_read, up(p - 1))
                    if is_zn:
                        act.wait_ge(n_read, up(p + 1))
                        nc.scalar.activation(n_sb[:, :], pre_n[:, :], ACT.Tanh, bias=bias_in[:, 4, o:o + 1])\
                            .then_inc(tanh_ready, 1)
                    act.wait_ge(rz_done, up(p + 1))
                    dst, b = (z_sb, bias_z) if is_zn else (r_sb, bias_r)
                    nc.scalar.activation(dst[:, :], rz[:, :], ACT.Sigmoid, bias=b[:, o:o + 1])\
                        .then_inc(rz_read, 1)
                if has_graph(i):
                    for b in range(2):
                        act.wait_ge((y0_done, y1_done)[b], up(i + 1))
                        nc.scalar.activation(y_hi[:, b * 512:(b + 1) * 512], y_bank[b][:, :], ACT.Copy)\
                            .then_inc((yhi0_ready, yhi1_ready)[b], 1)
                if has_graph(i + 1):
                    split_inputs(i + 1, up)
                if has_graph(i - 1):
                    act.wait_ge(out_done, up(i + 1))
                    src = out_bank[:, 0:H].rearrange("p (c n) -> p c n", c=HC)
                    nc.scalar.activation(oT_hi[:, ring(i - 1), :, cols(i - 1)], src, ACT.Relu)\
                        .then_inc(ohi_ready, 1)
                if i < HC:
                    act.wait_ge(wg_loaded[i], 16)
                    for t in range(WG_PIECES):
                        at = slice(t * 512, (t + 1) * 512)
                        nc.scalar.activation(wg_hi[:, i, at], wg_f[:, i, at], ACT.Copy).then_inc(wg_hi_ready, 1)
                p, o, is_zn = part_of(i)
                if has_graph(p) and p % GROUP == 0:
                    if p >= GROUP:
                        act.wait_ge(hn_ready, up(2 * (p // GROUP), 4))
                    nc.scalar.activation(x_keep[:, :, :], xT_f[:, ring(p), :, :], ACT.Copy)\
                        .then_inc(keep_ready, 1)

            run_steps(act, step)

        @block.vector
        def _(dve):
            def split_inputs(i, up):
                dve.wait_ge(xhi_ready, up(i + 1))
                nc.vector.tensor_tensor(xT_lo[:, ring(i), :, cols(i)], xT_f[:, ring(i), :, cols(i)],
                                        xT_hi[:, ring(i), :, cols(i)].bitcast(f32), ALU.subtract)\
                    .then_inc(xlo_ready, 1)

            def make_masks(i, up):
                if i >= 2:
                    dve.wait_ge(p_done, up(i - 1))
                labels_of = adjT_in[:, ring(i), cols(i)].unsqueeze(1).broadcast_to([128, D, N])
                nc.vector.tensor_tensor(masks[:, i % 2, :, :], labels_of, labels[:, :, :], ALU.is_equal)\
                    .then_inc(masks_ready, 1)

            for d in range(D):
                last = nc.vector.memset(labels[:, d, :], float(d + 1))
            last.then_inc(labels_ready, 1)
            split_inputs(0, lambda n, k=0: n)
            for b in range(2):
                for c in range(HC):
                    dve.wait_ge(wd_hi_ready, b * HC + c + 1)
                    at = slice(b * 512, (b + 1) * 512)
                    nc.vector.tensor_tensor(wd_lo[:, c, at], wd_f[:, c, at], wd_hi[:, c, at].bitcast(f32),
                                            ALU.subtract).then_inc(wd_ready, 1)
            dve.wait_ge(labels_ready, 1)
            make_masks(0, lambda n, k=0: n)
            dve.wait_ge(vec_loaded, 16 * 6)
            nc.vector.tensor_tensor(bias_r[:, :], bias_in[:, 0, :], bias_in[:, 1, :], ALU.add)\
                .then_inc(bias_ready, 1)
            nc.vector.tensor_tensor(bias_z[:, :], bias_in[:, 2, :], bias_in[:, 3, :], ALU.add)\
                .then_inc(bias_ready, 1)

            def step(i, up):
                p, o, is_zn = part_of(i - 1)
                if has_graph(p):
                    n_part = part_banks(p)[1]
                    if not is_zn:
                        dve.wait_ge(rz_read, up(p + 1))
                        nc.vector.scalar_tensor_tensor(rn_sb[:, :], n_part[:, :], bias_in[:, 5, o:o + 1],
                                                       r_sb[:, :], ALU.add, ALU.mult).then_inc(n_read, 1)
                    else:
                        dve.wait_ge(n_done, up(p + 1))
                        dve.wait_ge(n_read, up(p))
                        if p >= 2:
                            dve.wait_ge(tanh_ready, up((p - 1) // 2, 4))
                        nc.vector.tensor_tensor(pre_n[:, :], n_part[:, :], rn_sb[:, :], ALU.add)\
                            .then_inc(n_read, 1)
                if has_graph(i - 1):
                    dve.wait_ge(p_done, up(i))
                    for d in range(D):
                        dve.wait_ge(label_sum[d - 1] if d else rcount_ready, up(i))
                        nc.vector.scalar_tensor_tensor(
                            out_rows[:, :], p_bank[d // 2][:, (d % 2) * H:(d % 2 + 1) * H], rcount[:, d:d + 1],
                            out_rows[:, :] if d else bd_rows[:, :], ALU.mult, ALU.add).then_inc(label_sum[d], 1)
                j = i - LAG_STORE
                if has_graph(j):
                    dve.wait_ge(rstd_ready, up(j + 1))
                    dve.wait_ge(rows_read, up(j + 1))
                    if j >= GROUP:
                        dve.wait_ge(stored[j % GROUP], up(16 * (j // GROUP), 32))
                    nc.vector.scalar_tensor_tensor(normed[:, j % GROUP, :], centred[:, j % 2, :],
                                                   rstd[:, j % 2:j % 2 + 1], beta_rows[:, :],
                                                   ALU.mult, ALU.add).then_inc(norm_ready, 1)
                if has_graph(i):
                    for b in range(2):
                        dve.wait_ge((yhi0_ready, yhi1_ready)[b], up(i + 1))
                        at = slice(b * 512, (b + 1) * 512)
                        nc.vector.tensor_tensor(y_lo[:, at], y_bank[b][:, :], y_hi[:, at].bitcast(f32),
                                                ALU.subtract).then_inc((ylo0_ready, ylo1_ready)[b], 1)
                if has_graph(i + 1):
                    split_inputs(i + 1, up)
                    make_masks(i + 1, up)
                if i <= GRAPHS:
                    if i == 0:
                        dve.wait_ge(out_done, 1)
                    else:
                        dve.wait_ge(ohi_ready, up(i))
                if has_graph(i):
                    nc.vector.tensor_scalar(counts[:, :], out_bank[:, H:H + D], EPS, None, ALU.add)\
                        .then_inc(counts_ready, 1)
                if has_graph(i - 1):
                    src = out_bank[:, 0:H].rearrange("p (c n) -> p c n", c=HC)
                    nc.vector.scalar_tensor_tensor(oT_lo[:, ring(i - 1), :, cols(i - 1)], src, 0.0,
                                                   oT_hi[:, ring(i - 1), :, cols(i - 1)].bitcast(f32),
                                                   ALU.max, ALU.subtract).then_inc(olo_ready, 1)
                if has_graph(i):
                    dve.wait_ge(counts_ready, up(i + 1))
                    nc.vector.reciprocal(rcount[:, :], counts[:, :]).then_inc(rcount_ready, 1)
                if has_graph(p) and is_zn:
                    dve.wait_ge(hn_ready, up((p + 1) // 2, 4))
                    dve.wait_ge(rz_read, up(p + 1))
                    nc.vector.tensor_tensor(z_part[:, :], z_sb[:, :], h_minus_n[:, :], ALU.mult)\
                        .then_inc(zp_ready, 1)
                j = i - LAG_FINAL
                if has_graph(j):
                    dve.wait_ge(rows_done, up(j + 1))
                    nc.vector.bn_stats(stats[:, :], rows_bank(j)[:, 0:H]).then_inc(stats_ready, 1)
                if has_graph(p) and is_zn:
                    dve.wait_ge(zp_ready, up((p + 1) // 2, 4))
                    nc.vector.tensor_tensor(mixT[:, ring(p), o, :], z_part[:, :], n_sb[:, :], ALU.add)\
                        .then_inc(mix_ready, 1)
                if has_graph(j):
                    dve.wait_ge(vec_loaded, 16 * 6)
                    dve.wait_ge(stats_ready, up(j + 1))
                    nc.vector.bn_aggr(mean_var[:, j % 2, :], stats[:, :]).then_inc(mv_ready, 1)
                    dve.wait_ge(mv_ready, up(j + 1))
                    nc.vector.scalar_tensor_tensor(centred[:, j % 2, :], rows_bank(j)[:, 0:H],
                                                   mean_var[:, j % 2, 0:1], gamma_rows[:, :],
                                                   ALU.subtract, ALU.mult).then_inc(rows_read, 1)

            run_steps(dve, step)

        @block.gpsimd
        def _(pool):
            nc.gpsimd.memset(ones_bf[:, :], 1.0)
            nc.gpsimd.memset(ln_eps[:, :], LN_EPS)
            nc.gpsimd.memset(power[:, :], -0.5).then_inc(ident_zero, 1)
            nc.gpsimd.memset(ident[:, :], 0.0).then_inc(ident_zero, 1)
            pool.wait_ge(ident_zero, 2)
            nc.gpsimd.affine_select(out=ident[:, :], in_=ident[:, :], compare_op=ALU.not_equal, fill=1.0,
                                    base=0, pattern=[[-1, 128]], channel_multiplier=1).then_inc(const_ready, 1)

            for c in range(HC):
                for t in range(WG_PIECES):
                    pool.wait_ge(wg_hi_ready, c * WG_PIECES + t + 1)
                    at = slice(t * 512, (t + 1) * 512)
                    nc.gpsimd.tensor_tensor(wg_lo[:, c, at], wg_f[:, c, at], wg_hi[:, c, at].bitcast(f32),
                                            ALU.subtract).then_inc(wg_ready, 1)

            def step(i, up):
                p, o, is_zn = part_of(i - 1)
                if has_graph(p) and is_zn:
                    half = (p + 1) // 2
                    pool.wait_ge(tanh_ready, up(half, 4))
                    if half > 1:
                        pool.wait_ge(zp_ready, up(half - 1, 4))
                    if o == 0:
                        pool.wait_ge(keep_ready, up(p // GROUP + 1, 2))
                    nc.gpsimd.tensor_tensor(h_minus_n[:, :], x_keep[:, o, :], n_sb[:, :], ALU.subtract).then_inc(hn_ready, 1)
                j = i - LAG_FINAL
                if has_graph(j):
                    pool.wait_ge(mv_ready, up(j + 1))
                    nc.gpsimd.tensor_tensor(var_eps[:, :], mean_var[:, j % 2, 1:2], ln_eps[:, :], ALU.add)\
                        .then_inc(ve_ready, 1)
                    pool.wait_ge(ve_ready, up(j + 1))
                    nc.gpsimd.tensor_tensor(rstd[:, j % 2:j % 2 + 1], var_eps[:, :], power[:, :], ALU.pow)\
                        .then_inc(rstd_ready, 1)

            run_steps(pool, step)


def kernel(x, adj, L0_gnn_Wd, L0_gnn_bd, L0_gnn_Wri, L0_gnn_bri, L0_gnn_Wrh, L0_gnn_brh, L0_gnn_Wzi, L0_gnn_bzi,
           L0_gnn_Wzh, L0_gnn_bzh, L0_gnn_Wni, L0_gnn_bni, L0_gnn_Wnh, L0_gnn_bnh, L0_gnn_gamma, L0_gnn_beta):
    import numpy as np
    import concourse.bacc as bacc
    from concourse.bass_utils import run_bass_kernel_spmd

    def chunked(w):
        w = np.asarray(w)
        return w.T.reshape(HC, 128, w.shape[0]).transpose(1, 0, 2)

    def column(b):
        return np.asarray(b).reshape(HC, 128).T

    def pair(a, b):
        return np.ascontiguousarray(np.stack([column(a), column(b)], axis=1))

    xT = np.asarray(x).reshape(GRAPHS // GROUP, GROUP, N, HC, 128).transpose(0, 4, 3, 1, 2)
    xT = xT.reshape(GRAPHS // GROUP, 128, HC, COLS)
    adjT = np.asarray(adj).reshape(GRAPHS // GROUP, GROUP, N, N).transpose(0, 3, 1, 2)
    adjT = adjT.reshape(GRAPHS // GROUP, N, COLS)
    wd = np.asarray(L0_gnn_Wd).reshape(H, D, H)
    wdT = np.concatenate([chunked(wd[:, d, :]) for d in range(D)], axis=2)
    wgT = np.concatenate([chunked(w) for w in (L0_gnn_Wri, L0_gnn_Wzi, L0_gnn_Wni,
                                               L0_gnn_Wrh, L0_gnn_Wzh, L0_gnn_Wnh)], axis=2)
    arrays = {
        "xT": np.ascontiguousarray(xT), "adjT": np.ascontiguousarray(adjT),
        "wdT": np.ascontiguousarray(wdT), "wgT": np.ascontiguousarray(wgT),
        "bd": np.ascontiguousarray(L0_gnn_bd),
        "b_r": pair(L0_gnn_bri, L0_gnn_brh), "b_z": pair(L0_gnn_bzi, L0_gnn_bzh),
        "b_n": pair(L0_gnn_bni, L0_gnn_bnh),
        "gamma": np.ascontiguousarray(L0_gnn_gamma), "beta": np.ascontiguousarray(L0_gnn_beta),
    }
    nc = bacc.Bacc("TRN2", target_bir_lowering=False, num_devices=1)
    args = [nc.dram_tensor(f"in_{n}", a.shape, mybir.dt.from_np(a.dtype), kind="ExternalInput").ap()
            for n, a in arrays.items()]
    args.append(nc.dram_tensor("out", (GRAPHS, N, H), mybir.dt.float32, kind="ExternalOutput").ap())
    gnn_kernel(nc, *args)
    res = run_bass_kernel_spmd(nc, [{f"in_{n}": a for n, a in arrays.items()}], core_ids=[0])
    return res.results[0]["out"]
```

```python
import concourse.bass as bass
from concourse import mybir
from contextlib import ExitStack

GRAPHS, N, H, D = 64, 128, 256, 4
EPS, LN_EPS = 1e-8, 1e-5
GROUP = 4
RING = 2 * GROUP
HC = H // 128
LAG_GATES = 2
LAG_MIX = LAG_GATES + 1
LAG_STORE = LAG_MIX + 1
STEPS = GRAPHS + LAG_STORE
OT_RING = GROUP
BODY = RING
FIRST = 9
ROUNDS = 6
LAST = FIRST + ROUNDS * BODY
WG_PIECES = 3 * HC
TAIL = GRAPHS - 3


def gnn_kernel(nc, x, xT, adjT, wdT, wgT, bd, vectors, out):
    f32, f32r, bf16, i32 = mybir.dt.float32, mybir.dt.float32r, mybir.dt.bfloat16, mybir.dt.int32
    ALU, ACT = mybir.AluOpType, mybir.ActivationFunctionType

    ctx = ExitStack()
    with ctx:
        def sb(name, shape, dt=f32):
            return ctx.enter_context(nc.sbuf_tensor(name, shape, dt))

        def bank(name):
            return ctx.enter_context(nc.psum_tensor(name, [128, 512], f32))

        def sem(name):
            return ctx.enter_context(nc.semaphore(name))

        wd_f = sb("wd_f", [128, HC, D * H])
        wd_hi = sb("wd_hi", [128, HC, D * H], f32r)
        wd_lo = sb("wd_lo", [128, HC, D * H], f32r)
        wg_f = sb("wg_f", [128, HC, 6 * H])
        wg_hi = sb("wg_hi", [128, HC, 6 * H], f32r)
        wg_lo = sb("wg_lo", [128, HC, 6 * H], f32r)
        ident = sb("ident", [128, 128])
        ones_bf = sb("ones_bf", [128, 1], bf16)
        labels = sb("labels", [128, D, N])
        bd_rows = sb("bd_rows", [128, H])
        vec_rows = sb("vec_rows", [128, 8 * H])
        bni_rows, bnh_rows, gamma_rows, beta_rows = [slice(k * H, (k + 1) * H) for k in (4, 5, 6, 7)]
        bias_rz = sb("bias_rz", [128, 2 * H])
        power = sb("power", [128, 1])
        warm = sb("warm", [128, 1])
        ln_eps = sb("ln_eps", [128, 1])
        xT_f = sb("xT_f", [128, 2, HC, GROUP * N])
        adjT_in = sb("adjT_in", [128, 2, GROUP * N], i32)
        x_in = sb("x_in", [128, 2, GROUP, H])
        xT_hi = sb("xT_hi", [128, RING, HC, N], f32r)
        xT_lo = sb("xT_lo", [128, RING, HC, N], f32r)
        masks = sb("masks", [128, RING, D, N], f32r)
        y_hi = sb("y_hi", [128, D * H], f32r)
        y_lo = sb("y_lo", [128, D * H], f32r)
        counts = sb("counts", [128, RING * D])
        rcount = sb("rcount", [128, RING * D])
        out_rows = sb("out_rows", [128, H])
        oT_hi = sb("oT_hi", [128, OT_RING, HC, N], f32r)
        oT_lo = sb("oT_lo", [128, OT_RING, HC, N], f32r)
        rz_pre = sb("rz_pre", [128, 2 * H])
        rz_sb = sb("rz_sb", [128, 2, 2 * H])
        r_bnh = sb("r_bnh", [128, H])
        r_bias = sb("r_bias", [128, H])
        rn_sb = sb("rn_sb", [128, H])
        rn_sum = sb("rn_sum", [128, H])
        pre_n = sb("pre_n", [128, H])
        n_sb = sb("n_sb", [128, H])
        one_minus_z = sb("one_minus_z", [128, 2, H])
        z_h = sb("z_h", [128, 2, H])
        n_share = sb("n_share", [128, H])
        mix = sb("mix", [128, 2, H])
        stats = sb("stats", [128, 6])
        mean_var = sb("mean_var", [128, 2, 2])
        var_eps = sb("var_eps", [128, 1])
        rstd = sb("rstd", [128, 2])
        scaled = sb("scaled", [128, H])
        by_gamma = sb("by_gamma", [128, H])
        centred = sb("centred", [128, 2, H])
        normed = sb("normed", [128, GROUP, H])

        y_bank = [bank("y_bank0"), bank("y_bank1")]
        p_bank = [bank("p_bank0"), bank("p_bank1")]
        rz_bank = bank("rz_bank")
        n_bank = bank("n_bank")
        out_bank = bank("out_bank")
        count_bank = bank("count_bank")

        wd_loaded = [sem(f"wd_loaded{t}") for t in range(2 * HC)]
        wg_loaded = [sem(f"wg_loaded{c}") for c in range(HC)]
        bd_loaded = sem("bd_loaded")
        vec_loaded = sem("vec_loaded")
        ident_zero = sem("ident_zero")
        const_ready = sem("const_ready")
        labels_ready = sem("labels_ready")
        wd_hi_ready = sem("wd_hi_ready")
        wd_ready = sem("wd_ready")
        wg_hi_ready = sem("wg_hi_ready")
        wg_ready = sem("wg_ready")
        wg_last_ready = sem("wg_last_ready")
        bias_ready = sem("bias_ready")
        x0_loaded = sem("x0_loaded")
        adj0_loaded = sem("adj0_loaded")
        xT_loaded = [sem("xT_loaded0"), sem("xT_loaded1")]
        adj_loaded = [sem("adj_loaded0"), sem("adj_loaded1")]
        rows_loaded = [sem("rows_loaded0"), sem("rows_loaded1")]
        stored = [sem(f"stored{g}") for g in range(GROUP)]
        xhi_ready = sem("xhi_ready")
        xlo0_ready = sem("xlo0_ready")
        xlo_ready = sem("xlo_ready")
        masks_ready = sem("masks_ready")
        y_done = [sem("y0_done"), sem("y1_done")]
        yhi_ready = [sem("yhi0_ready"), sem("yhi1_ready")]
        ylo_ready = [sem("ylo0_ready"), sem("ylo1_ready")]
        p_done = sem("p_done")
        label_sum = [sem(f"label_sum{d}") for d in range(D)]
        count_done = sem("count_done")
        counts_ready = sem("counts_ready")
        rcount_ready = sem("rcount_ready")
        out_done = sem("out_done")
        ohi_ready = sem("ohi_ready")
        olo_ready = sem("olo_ready")
        rz_done = sem("rz_done")
        n_done = sem("n_done")
        rz_read = sem("rz_read")
        rz_ready = sem("rz_ready")
        r_bnh_ready = sem("r_bnh_ready")
        r_bias_ready = sem("r_bias_ready")
        rn_ready = sem("rn_ready")
        n_read = sem("n_read")
        pre_ready = sem("pre_ready")
        tanh_ready = sem("tanh_ready")
        mz_ready = sem("mz_ready")
        zh_ready = sem("zh_ready")
        share_ready = sem("share_ready")
        mix_ready = sem("mix_ready")
        stats_ready = sem("stats_ready")
        mv_ready = sem("mv_ready")
        ve_ready = sem("ve_ready")
        rstd_ready = sem("rstd_ready")
        norm_ready = sem("norm_ready")
        scaled_ready = sem("scaled_ready")
        result_ready = sem("result_ready")
        centred_ready = sem("centred_ready")

        def run_steps(eng, step):
            for i in range(FIRST):
                step(i, lambda n, k=BODY: n)
            with eng.Fori(0, ROUNDS) as rnd:
                for i in range(FIRST, FIRST + BODY):
                    step(i, lambda n, k=BODY: rnd * k + n)
            for i in range(LAST, STEPS):
                step(i, lambda n, k=BODY: n)

        def has_graph(i):
            return 0 <= i < GRAPHS

        def ring(graph):
            return (graph // GROUP) % 2

        def cols(graph):
            return slice((graph % GROUP) * N, (graph % GROUP + 1) * N)

        def half(b):
            return slice(b * 512, (b + 1) * 512)

        block = ctx.enter_context(nc.Block())

        def load_wd(eng, b, c):
            eng.dma_start(wd_f[:, c, half(b)], wdT[:, c, half(b)]).then_inc(wd_loaded[b * HC + c], 16)

        def masks_made(i):
            first, after = ahead(i), ahead(i + 1)
            return range(first, min(after, GRAPHS))

        def ahead(i):
            return i + 1 if i <= GROUP else min(i + GROUP, 2 * i - GROUP + 1)

        def counted(i):
            if i < 2 * GROUP:
                return range(i, i + 1)
            return range(i, i + GROUP) if i % GROUP == 0 and i < GRAPHS else range(0)

        def count_steps(i):
            return i + 1 if i < 2 * GROUP else 2 * GROUP + i // GROUP - 1

        def count_cols(i):
            return slice(i % RING * D, (i % RING + len(counted(i))) * D)

        def wg_piece(k):
            return k % HC, half((1, 0, 2)[k // HC])

        def split_lo(dst, full, hi):
            return dst, full, hi.bitcast(f32), ALU.subtract

        def xT_lo_of(i):
            return split_lo(xT_lo[:, i % RING, :, :], xT_f[:, ring(i), :, cols(i)], xT_hi[:, i % RING, :, :])

        def masks_of(i):
            labels_of = adjT_in[:, ring(i), cols(i)].unsqueeze(1).broadcast_to([128, D, N])
            return masks[:, i % RING, :, :], labels_of, labels[:, :, :], ALU.is_equal

        @block.sync
        def _(sp):
            def load_xT(k, index):
                sp.dma_start(xT_f[:, k % 2, :, :], xT[index]).then_inc(xT_loaded[k % 2], 16)

            def load_adj(k, index):
                sp.dma_start(adjT_in[:, k % 2, :], adjT[index]).then_inc(adj_loaded[k % 2], 16)

            def load_rows(k, index):
                sp.dma_start(x_in[:, k % 2, :, :], x[index].rearrange("g n h -> n g h"))\
                    .then_inc(rows_loaded[k % 2], 16)

            sp.dma_start(xT_f[:, 0, :, 0:N], xT[0, :, :, 0:N]).then_inc(x0_loaded, 16)
            load_wd(sp, 0, 0)
            load_wd(sp, 1, 0)
            load_wd(sp, 1, 1)
            sp.dma_start(xT_f[:, 0, :, N:GROUP * N], xT[0, :, :, N:GROUP * N]).then_inc(xT_loaded[0], 16)
            sp.dma_start(adjT_in[:, 0, N:GROUP * N], adjT[0, :, N:GROUP * N]).then_inc(adj_loaded[0], 16)
            sp.dma_start(bd_rows[:, :], bd.partition_broadcast(128)).then_inc(bd_loaded, 16)
            for c in range(HC):
                sp.dma_start(wg_f[:, c, :], wgT[:, c, :]).then_inc(wg_loaded[c], 16)
            load_xT(1, 1)
            load_adj(1, 1)
            sp.dma_start(vec_rows[:, :], vectors.partition_broadcast(128)).then_inc(vec_loaded, 16)
            load_rows(0, 0)
            load_rows(1, 1)

            def step(i, up):
                k = i // GROUP
                if i % GROUP == 1 and k >= 1 and (k + 1) * GROUP < GRAPHS:
                    sp.wait_ge(xlo_ready, up(k * GROUP - 1))
                    load_xT(k + 1, up(k + 1, 2))
                if i % GROUP == 1 and (k + 2) * GROUP < GRAPHS:
                    sp.wait_ge(masks_ready, up((k + 1) * GROUP))
                    load_adj(k % 2, up(k + 2, 2))
                if i % GROUP == 0 and 2 <= k < GRAPHS // GROUP:
                    sp.wait_ge(zh_ready, up((k - 1) * GROUP))
                    load_rows(k, up(k, 2))
                j = i - LAG_STORE
                if has_graph(j):
                    sp.wait_ge(result_ready, up(j + 1))
                    sp.dma_start(out[up(j)], normed[:, j % GROUP, :]).then_inc(stored[j % GROUP], 16)

            run_steps(sp, step)
            for g in range(GROUP):
                sp.wait_ge(stored[g], 16 * GRAPHS // GROUP)

        @block.tensor
        def _(pe):
            def passes(dst, hi, lo, w_at, w_hi, w_lo, first, final, before=None):
                for c in range(HC):
                    for t, (m, w) in enumerate([(hi, w_hi), (lo, w_hi), (hi, w_lo)]):
                        if before:
                            before(c, t)
                        last = nc.tensor.matmul(dst, m[:, c, :], w[:, c, w_at],
                                                start=(first and c == 0 and t == 0),
                                                stop=(final and c == HC - 1 and t == 2))
                return last

            pe.wait_ge(const_ready, 1)

            def step(i, up):
                g = i - LAG_GATES
                if has_graph(i):
                    if i == 0:
                        pe.wait_ge(xlo0_ready, 1)
                    else:
                        pe.wait_ge(xlo_ready, up(i))
                    x_hi, x_lo = xT_hi[:, i % RING, :, :], xT_lo[:, i % RING, :, :]
                    for b in range(2):
                        if i >= 1:
                            pe.wait_ge(ylo_ready[b], up(i))

                        def weights(c, t):
                            if t != 1:
                                pe.wait_ge(wd_ready if t else wd_hi_ready, b * HC + c + 1)

                        passes(y_bank[b][:, :], x_hi, x_lo, half(b), wd_hi, wd_lo, True, True,
                               before=weights if i == 0 else None).then_inc(y_done[b], 1)
                if counted(i):
                    pe.wait_ge(masks_ready, up(counted(i)[-1] + 1))
                    if i >= 1:
                        pe.wait_ge(counts_ready, up(count_steps(i) - 1, 2))
                    for k in counted(i):
                        halves = masks[:, k % RING, :, :].bitcast(bf16).rearrange("n d (m t) -> n d m t", t=2)
                        for d in range(D):
                            col = k % RING * D + d
                            last = nc.tensor.matmul(count_bank[:, col:col + 1], halves[:, d, :, 1],
                                                    ones_bf[:, :], start=True, stop=True)
                    last.then_inc(count_done, 1)
                if has_graph(g):
                    x_hi, x_lo = xT_hi[:, g % RING, :, :], xT_lo[:, g % RING, :, :]
                    o_hi, o_lo = oT_hi[:, g % OT_RING, :, :], oT_lo[:, g % OT_RING, :, :]
                    rz, n_part = (y_bank[0], p_bank[0]) if g == GRAPHS - 1 else (rz_bank, n_bank)

                    def need_pieces(k):
                        if g == 0:
                            pe.wait_ge(wg_ready, min(k, WG_PIECES - 1))
                            if k == WG_PIECES:
                                pe.wait_ge(wg_last_ready, 1)

                    need_pieces(HC)
                    if 0 < g < GRAPHS - 1:
                        pe.wait_ge(rz_read, up(g))
                    passes(rz[:, :], x_hi, x_lo, slice(2 * H, 4 * H), wg_hi, wg_lo, True, False)
                    need_pieces(2 * HC)
                    pe.wait_ge(olo_ready, up(g + 1))
                    passes(rz[:, :], o_hi, o_lo, slice(0, 2 * H), wg_hi, wg_lo, False, True)\
                        .then_inc(rz_done, 1)
                if has_graph(i - 1):
                    if i >= 2:
                        pe.wait_ge(olo_ready, up(i - 1))
                    pe.wait_ge(label_sum[D - 1], up(i))
                    for c in range(HC):
                        last = nc.tensor.transpose(out_bank[:, c * 128:(c + 1) * 128],
                                                   out_rows[:, c * 128:(c + 1) * 128], ident[:, :])
                    last.then_inc(out_done, 1)
                if has_graph(g):
                    need_pieces(3 * HC)
                    if 0 < g < GRAPHS - 1:
                        pe.wait_ge(n_read, up(g))
                    passes(n_part[:, 0:H], x_hi, x_lo, slice(5 * H, 6 * H), wg_hi, wg_lo, True, True)
                    passes(n_part[:, H:2 * H], o_hi, o_lo, slice(4 * H, 5 * H), wg_hi, wg_lo, True, True)\
                        .then_inc(n_done, 1)
                if has_graph(i):
                    for d in range(D):
                        if d % 2 == 0:
                            pe.wait_ge(ylo_ready[d // 2], up(i + 1))
                        for y in (y_hi, y_lo):
                            last = nc.tensor.matmul(p_bank[d // 2][:, (d % 2) * H:(d % 2 + 1) * H],
                                                    masks[:, i % RING, d, :], y[:, d * H:(d + 1) * H],
                                                    start=(y is y_hi), stop=(y is y_lo))
                    last.then_inc(p_done, 1)

            run_steps(pe, step)

        @block.scalar
        def _(act):
            def split_inputs(i, up):
                if i == 0:
                    act.wait_ge(x0_loaded, 16)
                elif i == 1 or i % GROUP == 0:
                    act.wait_ge(xT_loaded[ring(i)], up(16 * (i // RING + 1), 16))
                if i >= RING:
                    act.wait_ge(n_done, up(i - RING + 1))
                nc.scalar.activation(xT_hi[:, i % RING, :, :], xT_f[:, ring(i), :, cols(i)], ACT.Copy)\
                    .then_inc(xhi_ready, 1)

            act.wait_ge(ident_zero, 1)
            nc.scalar.activation(warm[:, :], power[:, :], ACT.Sigmoid)
            split_inputs(0, lambda n, k=0: n)
            for b in range(2):
                for c in range(HC):
                    act.wait_ge(wd_loaded[b * HC + c], 16)
                    nc.scalar.activation(wd_hi[:, c, half(b)], wd_f[:, c, half(b)], ACT.Copy)\
                        .then_inc(wd_hi_ready, 1)

            def step(i, up):
                g, h = i - LAG_GATES, i - LAG_MIX
                if has_graph(i + 1):
                    split_inputs(i + 1, up)
                if has_graph(i):
                    act.wait_ge(y_done[0], up(i + 1))
                    nc.scalar.activation(y_hi[:, half(0)], y_bank[0][:, :], ACT.Copy).then_inc(yhi_ready[0], 1)
                if has_graph(h):
                    act.wait_ge(pre_ready, up(h + 1))
                    if h >= 1:
                        act.wait_ge(mix_ready, up(h))
                    nc.scalar.activation(n_sb[:, :], pre_n[:, :], ACT.Tanh).then_inc(tanh_ready, 1)
                if has_graph(i):
                    act.wait_ge(y_done[1], up(i + 1))
                    nc.scalar.activation(y_hi[:, half(1)], y_bank[1][:, :], ACT.Copy).then_inc(yhi_ready[1], 1)
                if i < 3:
                    for k in range(i * HC, (i + 1) * HC):
                        c, at = wg_piece(k)
                        act.wait_ge(wg_loaded[c], 16)
                        nc.scalar.activation(wg_hi[:, c, at], wg_f[:, c, at], ACT.Copy).then_inc(wg_hi_ready, 1)
                if has_graph(i - 1):
                    act.wait_ge(out_done, up(i))
                    if i - 1 >= OT_RING:
                        act.wait_ge(n_done, up(i - OT_RING))
                    src = out_bank[:, 0:H].rearrange("p (c n) -> p c n", c=HC)
                    nc.scalar.activation(oT_hi[:, (i - 1) % OT_RING, :, :], src, ACT.Relu).then_inc(ohi_ready, 1)
                if has_graph(g):
                    act.wait_ge(rz_read, up(g + 1))
                    nc.scalar.activation(rz_sb[:, g % 2, :], rz_pre[:, :], ACT.Sigmoid).then_inc(rz_ready, 1)
                    nc.scalar.activation(one_minus_z[:, g % 2, :], rz_pre[:, H:2 * H], ACT.Sigmoid, scale=-1.0)\
                        .then_inc(mz_ready, 1)

            run_steps(act, step)

        @block.vector
        def _(dve):
            for d in range(D):
                last = nc.vector.memset(labels[:, d, :], float(d + 1))
            last.then_inc(labels_ready, 1)
            dve.wait_ge(xhi_ready, 1)
            nc.vector.tensor_tensor(*xT_lo_of(0)).then_inc(xlo0_ready, 1)
            for b in range(2):
                for c in range(HC):
                    dve.wait_ge(wd_hi_ready, b * HC + c + 1)
                    nc.vector.tensor_tensor(*split_lo(wd_lo[:, c, half(b)], wd_f[:, c, half(b)],
                                                      wd_hi[:, c, half(b)])).then_inc(wd_ready, 1)
            dve.wait_ge(labels_ready, 1)
            dve.wait_ge(adj0_loaded, 16)
            nc.vector.tensor_tensor(*masks_of(0)).then_inc(masks_ready, 1)

            def step(i, up):
                g, h, j = i - LAG_GATES, i - LAG_MIX, i - LAG_STORE

                def sum_label(d):
                    if d == 0:
                        dve.wait_ge(p_done, up(i))
                        if i >= 2:
                            dve.wait_ge(out_done, up(i - 1))
                        dve.wait_ge(rcount_ready, up(count_steps(i - 1), 2))
                    else:
                        dve.wait_ge(label_sum[d - 1], up(i))
                    col = (i - 1) % RING * D + d
                    nc.vector.scalar_tensor_tensor(
                        out_rows[:, :], p_bank[d // 2][:, (d % 2) * H:(d % 2 + 1) * H], rcount[:, col:col + 1],
                        out_rows[:, :] if d else bd_rows[:, :], ALU.mult, ALU.add).then_inc(label_sum[d], 1)

                n_part = p_bank[0] if h == GRAPHS - 1 else n_bank

                def times_r():
                    dve.wait_ge(n_done, up(h + 1))
                    dve.wait_ge(rz_ready, up(h + 1))
                    nc.vector.tensor_tensor(rn_sb[:, :], n_part[:, 0:H], rz_sb[:, h % 2, 0:H], ALU.mult)\
                        .then_inc(rn_ready, 1)

                def add_from_out():
                    if h >= 1:
                        dve.wait_ge(pre_ready, up(h))
                    dve.wait_ge(rn_ready, up(h + 1))
                    nc.vector.tensor_tensor(rn_sum[:, :], n_part[:, H:2 * H], rn_sb[:, :], ALU.add)\
                        .then_inc(n_read, 1)

                def add_bias():
                    dve.wait_ge(tanh_ready, h)
                    dve.wait_ge(r_bias_ready, h + 1)
                    dve.wait_ge(n_read, h + 1)
                    nc.vector.tensor_tensor(pre_n[:, :], rn_sum[:, :], r_bias[:, :], ALU.add)\
                        .then_inc(pre_ready, 1)

                chain = [times_r, add_from_out] + ([None, add_bias] if h >= TAIL else [])
                if i == 1:
                    dve.wait_ge(bd_loaded, 16)
                for d in range(D):
                    if has_graph(i - 1):
                        sum_label(d)
                    if has_graph(h) and d < len(chain) and chain[d]:
                        chain[d]()
                if has_graph(j) and j < TAIL:
                    dve.wait_ge(rstd_ready, up(j + 1))
                    if j >= 1:
                        dve.wait_ge(scaled_ready, up(j))
                    nc.vector.tensor_scalar(scaled[:, :], mix[:, j % 2, :], mean_var[:, j % 2, 0:1],
                                            rstd[:, j % 2:j % 2 + 1], ALU.subtract, ALU.mult)\
                        .then_inc(norm_ready, 1)

                def add_bias_rz():
                    if g == 0:
                        dve.wait_ge(bias_ready, 1)
                    else:
                        dve.wait_ge(mz_ready, up(g))
                    dve.wait_ge(rz_done, up(g + 1))
                    rz = y_bank[0] if g == GRAPHS - 1 else rz_bank
                    nc.vector.tensor_tensor(rz_pre[:, :], rz[:, :], bias_rz[:, :], ALU.add)\
                        .then_inc(rz_read, 1)

                if has_graph(g) and i >= GRAPHS:
                    add_bias_rz()

                def make_masks():
                    for k in masks_made(i):
                        if k == 1 or k % GROUP == 0:
                            dve.wait_ge(adj_loaded[ring(k)], up(16 * (k // RING + 1), 16))
                        nc.vector.tensor_tensor(*masks_of(k)).then_inc(masks_ready, 1)

                for b in range(2):
                    if has_graph(i):
                        dve.wait_ge(yhi_ready[b], up(i + 1))
                        nc.vector.tensor_tensor(*split_lo(y_lo[:, half(b)], y_bank[b][:, :], y_hi[:, half(b)]))\
                            .then_inc(ylo_ready[b], 1)
                    if b == (i < 2):
                        make_masks()
                if counted(i):
                    dve.wait_ge(count_done, up(count_steps(i), 2))
                    nc.vector.tensor_scalar(counts[:, count_cols(i)], count_bank[:, count_cols(i)], EPS, None,
                                            ALU.add).then_inc(counts_ready, 1)
                if has_graph(h):
                    dve.wait_ge(mz_ready, up(h + 1))
                    dve.wait_ge(tanh_ready, up(h + 1))
                    nc.vector.tensor_tensor(n_share[:, :], one_minus_z[:, h % 2, :], n_sb[:, :], ALU.mult)\
                        .then_inc(share_ready, 1)
                if counted(i):
                    dve.wait_ge(counts_ready, up(count_steps(i), 2))
                    nc.vector.reciprocal(rcount[:, count_cols(i)], counts[:, count_cols(i)])\
                        .then_inc(rcount_ready, 1)
                if has_graph(h):
                    dve.wait_ge(zh_ready, up(h + 1))
                    dve.wait_ge(share_ready, up(h + 1))
                    nc.vector.tensor_tensor(mix[:, h % 2, :], n_share[:, :], z_h[:, h % 2, :], ALU.add)\
                        .then_inc(mix_ready, 1)
                if i == 2:
                    c, at = wg_piece(WG_PIECES - 1)
                    dve.wait_ge(wg_hi_ready, WG_PIECES)
                    nc.vector.tensor_tensor(*split_lo(wg_lo[:, c, at], wg_f[:, c, at], wg_hi[:, c, at]))\
                        .then_inc(wg_last_ready, 1)
                if has_graph(i - 1):
                    dve.wait_ge(ohi_ready, up(i))
                    src = out_bank[:, 0:H].rearrange("p (c n) -> p c n", c=HC)
                    nc.vector.scalar_tensor_tensor(oT_lo[:, (i - 1) % OT_RING, :, :], src, 0.0,
                                                   oT_hi[:, (i - 1) % OT_RING, :, :].bitcast(f32),
                                                   ALU.max, ALU.subtract).then_inc(olo_ready, 1)
                if has_graph(h):
                    dve.wait_ge(mix_ready, up(h + 1))
                    nc.vector.bn_stats(stats[:, :], mix[:, h % 2, :]).then_inc(stats_ready, 1)
                if has_graph(j) and j >= TAIL:
                    dve.wait_ge(stored[j % GROUP], 16 * (j // GROUP))
                    dve.wait_ge(centred_ready, j - TAIL + 1)
                    dve.wait_ge(rstd_ready, j + 1)
                    nc.vector.scalar_tensor_tensor(normed[:, j % GROUP, :], centred[:, j % 2, :],
                                                   rstd[:, j % 2:j % 2 + 1], vec_rows[:, beta_rows],
                                                   ALU.mult, ALU.add).then_inc(result_ready, 1)
                if i == LAG_GATES:
                    dve.wait_ge(vec_loaded, 16)
                    nc.vector.tensor_tensor(bias_rz[:, :], vec_rows[:, 0:2 * H], vec_rows[:, 2 * H:4 * H],
                                            ALU.add).then_inc(bias_ready, 1)
                if has_graph(g) and i < GRAPHS:
                    add_bias_rz()
                if has_graph(h):
                    dve.wait_ge(vec_loaded, 16)
                    dve.wait_ge(stats_ready, up(h + 1))
                    nc.vector.bn_aggr(mean_var[:, h % 2, :], stats[:, :]).then_inc(mv_ready, 1)
                if has_graph(h) and h >= TAIL:
                    dve.wait_ge(mv_ready, h + 1)
                    nc.vector.scalar_tensor_tensor(centred[:, h % 2, :], mix[:, h % 2, :],
                                                   mean_var[:, h % 2, 0:1], vec_rows[:, gamma_rows],
                                                   ALU.subtract, ALU.mult).then_inc(centred_ready, 1)

            run_steps(dve, step)

        @block.gpsimd
        def _(pool):
            nc.gpsimd.memset(ones_bf[:, :], 1.0)
            nc.gpsimd.memset(ln_eps[:, :], LN_EPS)
            nc.gpsimd.memset(power[:, :], -0.5).then_inc(ident_zero, 1)
            nc.gpsimd.memset(ident[:, :], 0.0).then_inc(ident_zero, 1)
            load_wd(pool, 0, 1)
            pool.dma_start(adjT_in[:, 0, 0:N], adjT[0, :, 0:N]).then_inc(adj0_loaded, 16)
            pool.wait_ge(ident_zero, 2)
            nc.gpsimd.affine_select(out=ident[:, :], in_=ident[:, :], compare_op=ALU.not_equal, fill=1.0,
                                    base=0, pattern=[[-1, 128]], channel_multiplier=1).then_inc(const_ready, 1)
            pool.wait_ge(labels_ready, 1)

            def step(i, up):
                g, h, j = i - LAG_GATES, i - LAG_MIX, i - LAG_STORE
                if has_graph(h) and h < TAIL:
                    if h >= 1:
                        pool.wait_ge(tanh_ready, up(h))
                    pool.wait_ge(r_bias_ready, up(h + 1))
                    pool.wait_ge(n_read, up(h + 1))
                    nc.gpsimd.tensor_tensor(pre_n[:, :], rn_sum[:, :], r_bias[:, :], ALU.add)\
                        .then_inc(pre_ready, 1)
                if has_graph(i + 1):
                    pool.wait_ge(xhi_ready, up(i + 2))
                    nc.gpsimd.tensor_tensor(*xT_lo_of(i + 1)).then_inc(xlo_ready, 1)
                if i < 3:
                    for k in range(i * HC, min((i + 1) * HC, WG_PIECES - 1)):
                        c, at = wg_piece(k)
                        pool.wait_ge(wg_hi_ready, k + 1)
                        nc.gpsimd.tensor_tensor(*split_lo(wg_lo[:, c, at], wg_f[:, c, at], wg_hi[:, c, at]))\
                            .then_inc(wg_ready, 1)
                if has_graph(j) and j < TAIL:
                    pool.wait_ge(norm_ready, up(j + 1))
                    if j >= 1:
                        pool.wait_ge(result_ready, up(j))
                    nc.gpsimd.tensor_tensor(by_gamma[:, :], scaled[:, :], vec_rows[:, gamma_rows], ALU.mult)\
                        .then_inc(scaled_ready, 1)
                    if j >= GROUP:
                        pool.wait_ge(stored[j % GROUP], up(16 * (j // GROUP), 32))
                    pool.wait_ge(scaled_ready, up(j + 1))
                    nc.gpsimd.tensor_tensor(normed[:, j % GROUP, :], by_gamma[:, :], vec_rows[:, beta_rows],
                                            ALU.add).then_inc(result_ready, 1)

                def inverse_deviation():
                    pool.wait_ge(mv_ready, up(h + 1))
                    nc.gpsimd.tensor_tensor(var_eps[:, :], mean_var[:, h % 2, 1:2], ln_eps[:, :], ALU.add)\
                        .then_inc(ve_ready, 1)
                    if 2 <= h < TAIL + 2:
                        pool.wait_ge(norm_ready, up(h - 1))
                    pool.wait_ge(ve_ready, up(h + 1))
                    nc.gpsimd.tensor_tensor(rstd[:, h % 2:h % 2 + 1], var_eps[:, :], power[:, :], ALU.pow)\
                        .then_inc(rstd_ready, 1)

                def gate_terms():
                    if g == 0:
                        pool.wait_ge(vec_loaded, 16)
                    pool.wait_ge(rz_ready, up(g + 1))
                    nc.gpsimd.tensor_tensor(r_bnh[:, :], rz_sb[:, g % 2, 0:H], vec_rows[:, bnh_rows], ALU.mult)\
                        .then_inc(r_bnh_ready, 1)
                    if g >= 1:
                        pool.wait_ge(pre_ready, up(g))
                    pool.wait_ge(r_bnh_ready, up(g + 1))
                    nc.gpsimd.tensor_tensor(r_bias[:, :], r_bnh[:, :], vec_rows[:, bni_rows], ALU.add)\
                        .then_inc(r_bias_ready, 1)
                    if g % GROUP == 0:
                        pool.wait_ge(rows_loaded[ring(g)], up(16 * (g // RING + 1), 16))
                    if g >= 2:
                        pool.wait_ge(mix_ready, up(g - 1))
                    nc.gpsimd.tensor_tensor(z_h[:, g % 2, :], rz_sb[:, g % 2, H:2 * H],
                                            x_in[:, ring(g), g % GROUP, :], ALU.mult).then_inc(zh_ready, 1)

                for part in (gate_terms, inverse_deviation) if i >= GRAPHS else (inverse_deviation, gate_terms):
                    if has_graph(g if part is gate_terms else h):
                        part()

            run_steps(pool, step)


def kernel(x, adj, L0_gnn_Wd, L0_gnn_bd, L0_gnn_Wri, L0_gnn_bri, L0_gnn_Wrh, L0_gnn_brh, L0_gnn_Wzi, L0_gnn_bzi,
           L0_gnn_Wzh, L0_gnn_bzh, L0_gnn_Wni, L0_gnn_bni, L0_gnn_Wnh, L0_gnn_bnh, L0_gnn_gamma, L0_gnn_beta):
    import numpy as np
    import concourse.bacc as bacc
    from concourse.bass_utils import run_bass_kernel_spmd

    def chunked(w):
        w = np.asarray(w)
        return w.T.reshape(HC, 128, w.shape[0]).transpose(1, 0, 2)

    xT = np.asarray(x).reshape(GRAPHS // GROUP, GROUP, N, HC, 128).transpose(0, 4, 3, 1, 2)
    xT = xT.reshape(GRAPHS // GROUP, 128, HC, GROUP * N)
    adjT = np.asarray(adj).reshape(GRAPHS // GROUP, GROUP, N, N).transpose(0, 3, 1, 2)
    adjT = adjT.reshape(GRAPHS // GROUP, N, GROUP * N)
    wd = np.asarray(L0_gnn_Wd).reshape(H, D, H)
    wdT = np.concatenate([chunked(wd[:, d, :]) for d in range(D)], axis=2)
    wgT = np.concatenate([chunked(w) for w in (L0_gnn_Wri, L0_gnn_Wzi, L0_gnn_Wrh, L0_gnn_Wzh,
                                               L0_gnn_Wni, L0_gnn_Wnh)], axis=2)
    vectors = np.concatenate([np.asarray(v) for v in (L0_gnn_bri, L0_gnn_bzi, L0_gnn_brh, L0_gnn_bzh,
                                                      L0_gnn_bni, L0_gnn_bnh, L0_gnn_gamma, L0_gnn_beta)])
    arrays = {
        "x": np.ascontiguousarray(np.asarray(x).reshape(GRAPHS // GROUP, GROUP, N, H)),
        "xT": np.ascontiguousarray(xT), "adjT": np.ascontiguousarray(adjT),
        "wdT": np.ascontiguousarray(wdT), "wgT": np.ascontiguousarray(wgT),
        "bd": np.ascontiguousarray(L0_gnn_bd), "vectors": vectors,
    }
    nc = bacc.Bacc("TRN2", target_bir_lowering=False, num_devices=1)
    args = [nc.dram_tensor(f"in_{n}", a.shape, mybir.dt.from_np(a.dtype), kind="ExternalInput").ap()
            for n, a in arrays.items()]
    args.append(nc.dram_tensor("out", (GRAPHS, N, H), mybir.dt.float32, kind="ExternalOutput").ap())
    gnn_kernel(nc, *args)
    res = run_bass_kernel_spmd(nc, [{f"in_{n}": a for n, a in arrays.items()}], core_ids=[0])
    return res.results[0]["out"]
```
